# Optimizing a Trainium2 kernel written in Bass

```python
import numpy as np
import jax
import jax.numpy as jnp

def _softmax(x, axis=-1):
    return jax.nn.softmax(x, axis=axis)

def _gelu(x):
    return jax.nn.gelu(x, approximate=True)

def _silu(x):
    return jax.nn.silu(x)

def _sigmoid(x):
    return jax.nn.sigmoid(x)

def _layernorm(x, axis=-1, eps=1e-05):
    m = jnp.mean(x, axis=axis, keepdims=True)
    v = jnp.var(x, axis=axis, keepdims=True)
    return (x - m) / jnp.sqrt(v + eps)

def _scatter_add(tgt, idx, src, axis=0):
    return tgt.at[idx].add(src)

def _segment_sum(src, seg, n):
    return jax.ops.segment_sum(src, seg, n)
kernel_name = 'mk_xattn_seq_d2_seqx_r4_9b0c7c'

def setup_inputs(seed: int=0):
    np.random.seed(seed)
    _w = jnp.asarray

    def _rec_inputs():
        import jax
        import jax.numpy as jnp
        _rk = jax.random.key(seed)
        x = -0.0002928 + 1 * jax.random.normal(jax.random.fold_in(_rk, 1), (16, 256, 256), jnp.float32)
        _lenS = 256 - jax.random.randint(jax.random.fold_in(_rk, 7), (16,), 0, max(1, 256 // 4) + 1, jnp.int32)
        _lenS2 = 77 - jax.random.randint(jax.random.fold_in(_rk, 8), (16,), 0, max(1, 77 // 4) + 1, jnp.int32)
        _ctx_1024P = jax.random.normal(jax.random.fold_in(_rk, 11), (16, 16, 256), jnp.float32)
        _ctx_1024c = jax.random.dirichlet(jax.random.fold_in(_rk, 511), 0.3 * jnp.ones((16,), jnp.float32), (16, 77))
        _ctx_1024t = jnp.einsum('bsk,bkd->bsd', _ctx_1024c, _ctx_1024P)
        _ctx_1024t = _ctx_1024t * jax.lax.rsqrt(jnp.mean(jnp.square(_ctx_1024t)) + 1e-12) * 0.953939
        ctx_1024 = -1.39393e-06 + 0.999914 * (_ctx_1024t + 0.3 * jax.random.normal(jax.random.fold_in(_rk, 611), (16, 77, 256), jnp.float32))
        _validS = jnp.arange(256)[None, :] < _lenS[:, None]
        _validS2 = jnp.arange(77)[None, :] < _lenS2[:, None]
        _causal = jnp.tril(jnp.ones((256, 256), dtype=bool))
        mask_BxS_ff1 = jnp.where(jnp.ones((16, 256), dtype=bool), 1.0, 0.0).astype(jnp.float32)
        return (x, ctx_1024, mask_BxS_ff1)
    x, ctx_1024, mask_BxS_ff1 = _rec_inputs()

    def _L0_xattn_setup():
        import jax, jax.numpy as jnp
        import numpy as np
        D_MODEL = 256
        N_HEADS = 16
        D_HIDDEN = 1024
        EPS = 1e-06
        MASK_VAL = 10000000000.0

        def layernorm(x, gamma, beta):
            mean = jnp.mean(x, axis=-1, keepdims=True)
            d = x.shape[-1]
            std = jnp.sqrt(jnp.sum((x - mean) ** 2, axis=-1, keepdims=True) / (d - 1))
            return gamma * (x - mean) / (std + EPS) + beta

        def multihead(q_in, k_in, v_in, wq, wk, wv, wo, causal):
            q = q_in @ wq.T
            k = k_in @ wk.T
            v = v_in @ wv.T
            B, Sq, D = q.shape
            Sk = k.shape[1]
            H, dh = (N_HEADS, D // N_HEADS)
            q = q.reshape(B, Sq, H, dh)
            k = k.reshape(B, Sk, H, dh)
            v = v.reshape(B, Sk, H, dh)
            scores = jnp.einsum('bqhd,bkhd->bhqk', q, k)
            if causal:
                tri = jnp.triu(jnp.full((Sk, Sk), MASK_VAL, dtype=scores.dtype), k=1)
                scores = scores - tri
            scale = jnp.sqrt(jnp.asarray(D_MODEL, dtype=scores.dtype))
            att = jax.nn.softmax(scores / scale, axis=-1)
            out = jnp.einsum('bhqk,bkhd->bqhd', att, v).reshape(B, Sq, D)
            return out @ wo.T
        key = jax.random.key(seed)
        ks = jax.random.split(key, 24)
        B, S, D, DH = (2, 512, D_MODEL, D_HIDDEN)
        w = lambda k, shp: jax.random.normal(k, shp, dtype=jnp.float32) * 0.02
        inp = {'x': jax.random.normal(ks[0], (B, S, D), dtype=jnp.float32), 'encoding': jax.random.normal(ks[1], (B, S, D), dtype=jnp.float32), 'sa_wq': w(ks[2], (D, D)), 'sa_wk': w(ks[3], (D, D)), 'sa_wv': w(ks[4], (D, D)), 'sa_wo': w(ks[5], (D, D)), 'ca_wq': w(ks[6], (D, D)), 'ca_wk': w(ks[7], (D, D)), 'ca_wv': w(ks[8], (D, D)), 'ca_wo': w(ks[9], (D, D)), 'ff_w1': w(ks[10], (DH, D)), 'ff_b1': jnp.zeros((DH,), jnp.float32), 'ff_w2': w(ks[11], (D, DH)), 'ff_b2': jnp.zeros((D,), jnp.float32), 'ln1_g': jnp.ones((D,), jnp.float32), 'ln1_b': jnp.zeros((D,), jnp.float32), 'ln2_g': jnp.ones((D,), jnp.float32), 'ln2_b': jnp.zeros((D,), jnp.float32), 'ln3_g': jnp.ones((D,), jnp.float32), 'ln3_b': jnp.zeros((D,), jnp.float32)}
        return inp
    _L0_xattn_all = _L0_xattn_setup()
    _L0_xattn_in = {k: v for k, v in _L0_xattn_all.items() if k in ('sa_wq', 'sa_wk', 'sa_wv', 'sa_wo', 'ca_wq', 'ca_wk', 'ca_wv', 'ca_wo', 'ff_w1', 'ff_b1', 'ff_w2', 'ff_b2', 'ln1_g', 'ln1_b', 'ln2_g', 'ln2_b', 'ln3_g', 'ln3_b')}
    del _L0_xattn_all

    def _L1_xattn_setup():
        import jax, jax.numpy as jnp
        import numpy as np
        B, L, D = (8, 512, 256)
        key = jax.random.key(seed)
        ks = jax.random.split(key, 12)
        s = 1.0 / np.sqrt(D)
        return {'q': jax.random.normal(ks[0], (B, L, D), jnp.float32), 'k': jax.random.normal(ks[1], (B, L, D), jnp.float32), 'v': jax.random.normal(ks[2], (B, L, D), jnp.float32), 'mask': jnp.ones((B, L), jnp.float32), 'Wq': jax.random.normal(ks[3], (D, D), jnp.float32) * s, 'bq': jnp.zeros((D,), jnp.float32), 'Wk': jax.random.normal(ks[4], (D, D), jnp.float32) * s, 'bk': jnp.zeros((D,), jnp.float32), 'Wv': jax.random.normal(ks[5], (D, D), jnp.float32) * s, 'bv': jnp.zeros((D,), jnp.float32), 'Wg': jax.random.normal(ks[6], (2 * D, D), jnp.float32) * (1.0 / np.sqrt(2 * D)), 'bg': jnp.zeros((D,), jnp.float32)}
    _L1_xattn_all = _L1_xattn_setup()
    _L1_xattn_in = {k: v for k, v in _L1_xattn_all.items() if k in ('Wq', 'bq', 'Wk', 'bk', 'Wv', 'bv', 'Wg', 'bg')}
    del _L1_xattn_all
    return {'x': x, 'ctx_1024': ctx_1024, 'mask_BxS_ff1': mask_BxS_ff1, 'L0_xattn_sa_wq': _L0_xattn_in['sa_wq'], 'L0_xattn_sa_wk': _L0_xattn_in['sa_wk'], 'L0_xattn_sa_wv': _L0_xattn_in['sa_wv'], 'L0_xattn_sa_wo': _L0_xattn_in['sa_wo'], 'L0_xattn_ca_wq': _L0_xattn_in['ca_wq'], 'L0_xattn_ca_wk': _L0_xattn_in['ca_wk'], 'L0_xattn_ca_wv': _L0_xattn_in['ca_wv'], 'L0_xattn_ca_wo': _L0_xattn_in['ca_wo'], 'L0_xattn_ff_w1': _L0_xattn_in['ff_w1'], 'L0_xattn_ff_b1': _L0_xattn_in['ff_b1'], 'L0_xattn_ff_w2': _L0_xattn_in['ff_w2'], 'L0_xattn_ff_b2': _L0_xattn_in['ff_b2'], 'L0_xattn_ln1_g': _L0_xattn_in['ln1_g'], 'L0_xattn_ln1_b': _L0_xattn_in['ln1_b'], 'L0_xattn_ln2_g': _L0_xattn_in['ln2_g'], 'L0_xattn_ln2_b': _L0_xattn_in['ln2_b'], 'L0_xattn_ln3_g': _L0_xattn_in['ln3_g'], 'L0_xattn_ln3_b': _L0_xattn_in['ln3_b'], 'L1_xattn_Wq': _L1_xattn_in['Wq'], 'L1_xattn_bq': _L1_xattn_in['bq'], 'L1_xattn_Wk': _L1_xattn_in['Wk'], 'L1_xattn_bk': _L1_xattn_in['bk'], 'L1_xattn_Wv': _L1_xattn_in['Wv'], 'L1_xattn_bv': _L1_xattn_in['bv'], 'L1_xattn_Wg': _L1_xattn_in['Wg'], 'L1_xattn_bg': _L1_xattn_in['bg']}

def reference(x, ctx_1024, mask_BxS_ff1, L0_xattn_sa_wq, L0_xattn_sa_wk, L0_xattn_sa_wv, L0_xattn_sa_wo, L0_xattn_ca_wq, L0_xattn_ca_wk, L0_xattn_ca_wv, L0_xattn_ca_wo, L0_xattn_ff_w1, L0_xattn_ff_b1, L0_xattn_ff_w2, L0_xattn_ff_b2, L0_xattn_ln1_g, L0_xattn_ln1_b, L0_xattn_ln2_g, L0_xattn_ln2_b, L0_xattn_ln3_g, L0_xattn_ln3_b, L1_xattn_Wq, L1_xattn_bq, L1_xattn_Wk, L1_xattn_bk, L1_xattn_Wv, L1_xattn_bv, L1_xattn_Wg, L1_xattn_bg):
    import jax
    import jax.numpy as jnp

    def _L0_xattn_ref(x, encoding, sa_wq, sa_wk, sa_wv, sa_wo, ca_wq, ca_wk, ca_wv, ca_wo, ff_w1, ff_b1, ff_w2, ff_b2, ln1_g, ln1_b, ln2_g, ln2_b, ln3_g, ln3_b):
        import jax, jax.numpy as jnp
        import numpy as np
        D_MODEL = 256
        N_HEADS = 16
        D_HIDDEN = 1024
        EPS = 1e-06
        MASK_VAL = 10000000000.0

        def layernorm(x, gamma, beta):
            mean = jnp.mean(x, axis=-1, keepdims=True)
            d = x.shape[-1]
            std = jnp.sqrt(jnp.sum((x - mean) ** 2, axis=-1, keepdims=True) / (d - 1))
            return gamma * (x - mean) / (std + EPS) + beta

        def multihead(q_in, k_in, v_in, wq, wk, wv, wo, causal):
            q = q_in @ wq.T
            k = k_in @ wk.T
            v = v_in @ wv.T
            B, Sq, D = q.shape
            Sk = k.shape[1]
            H, dh = (N_HEADS, D // N_HEADS)
            q = q.reshape(B, Sq, H, dh)
            k = k.reshape(B, Sk, H, dh)
            v = v.reshape(B, Sk, H, dh)
            scores = jnp.einsum('bqhd,bkhd->bhqk', q, k)
            if causal:
                tri = jnp.triu(jnp.full((Sk, Sk), MASK_VAL, dtype=scores.dtype), k=1)
                scores = scores - tri
            scale = jnp.sqrt(jnp.asarray(D_MODEL, dtype=scores.dtype))
            att = jax.nn.softmax(scores / scale, axis=-1)
            out = jnp.einsum('bhqk,bkhd->bqhd', att, v).reshape(B, Sq, D)
            return out @ wo.T
        h = layernorm(x + multihead(x, x, x, sa_wq, sa_wk, sa_wv, sa_wo, causal=True), ln1_g, ln1_b)
        h = layernorm(h + multihead(h, encoding, encoding, ca_wq, ca_wk, ca_wv, ca_wo, causal=False), ln2_g, ln2_b)
        ff = jax.nn.relu(h @ ff_w1.T + ff_b1) @ ff_w2.T + ff_b2
        return layernorm(h + ff, ln3_g, ln3_b)

    def _L1_xattn_ref(q, k, v, mask, Wq, bq, Wk, bk, Wv, bv, Wg, bg):
        import jax, jax.numpy as jnp
        import numpy as np
        B, L, D = (8, 512, 256)
        q0 = q
        qp = q @ Wq + bq
        kp = k @ Wk + bk
        vp = v @ Wv + bv
        scale = 1.0 / jnp.sqrt(jnp.asarray(qp.shape[-1], qp.dtype))
        w = jnp.einsum('bqd,bkd->bqk', qp, kp) * scale
        w = jax.nn.softmax(w, axis=-1)
        x = jnp.einsum('bqk,bkd->bqd', w, vp)
        gate = jnp.concatenate((qp, x), axis=-1) @ Wg + bg
        x = x * mask[..., None]
        x = x * jax.nn.sigmoid(gate)
        return x + q0
    x = _L0_xattn_ref(x, ctx_1024, L0_xattn_sa_wq, L0_xattn_sa_wk, L0_xattn_sa_wv, L0_xattn_sa_wo, L0_xattn_ca_wq, L0_xattn_ca_wk, L0_xattn_ca_wv, L0_xattn_ca_wo, L0_xattn_ff_w1, L0_xattn_ff_b1, L0_xattn_ff_w2, L0_xattn_ff_b2, L0_xattn_ln1_g, L0_xattn_ln1_b, L0_xattn_ln2_g, L0_xattn_ln2_b, L0_xattn_ln3_g, L0_xattn_ln3_b)
    x = _L1_xattn_ref(x, ctx_1024, ctx_1024, mask_BxS_ff1, L1_xattn_Wq, L1_xattn_bq, L1_xattn_Wk, L1_xattn_bk, L1_xattn_Wv, L1_xattn_bv, L1_xattn_Wg, L1_xattn_bg)
    return x

_drawn_inputs = setup_inputs


def setup_inputs(seed=0):
    import zlib

    import numpy as np

    out = dict(_drawn_inputs(seed))
    spreads = {'L0_xattn_ff_b1': (0.0, 0.1),
     'L0_xattn_ff_b2': (0.0, 0.1),
     'L0_xattn_ln1_g': (1.0, 0.2),
     'L0_xattn_ln1_b': (0.0, 0.1),
     'L0_xattn_ln2_g': (1.0, 0.2),
     'L0_xattn_ln2_b': (0.0, 0.1),
     'L0_xattn_ln3_g': (1.0, 0.2),
     'L0_xattn_ln3_b': (0.0, 0.1),
     'L1_xattn_bq': (0.0, 0.574),
     'L1_xattn_bk': (0.0, 0.8),
     'L1_xattn_bv': (0.0, 0.1),
     'L1_xattn_bg': (0.0, 0.714)}
    factors = {'L0_xattn_sa_wq': 8.0,
     'L0_xattn_sa_wk': 8.0,
     'L0_xattn_sa_wv': 3.727,
     'L0_xattn_sa_wo': 3.755,
     'L0_xattn_ca_wq': 8.0,
     'L0_xattn_ca_wk': 8.0}
    for name, (base, spread) in spreads.items():
        noise = np.random.default_rng([zlib.crc32(name.encode()), seed]).standard_normal(out[name].shape)
        drawn = base * np.exp(spread * noise) if base else spread * noise
        out[name] = jnp.asarray(drawn.astype(out[name].dtype))
    for name, factor in factors.items():
        out[name] = (out[name] * factor).astype(out[name].dtype)
    return out
```

```python
from contextlib import ExitStack

import concourse.bass as bass
from concourse import mybir

F32 = mybir.dt.float32
F32R = mybir.dt.float32r
BF16 = mybir.dt.bfloat16
ACT = mybir.ActivationFunctionType
ALU = mybir.AluOpType
AX = mybir.AxisListType

P = 128
B = 16
S = 256
SC = 77
D = 256
H = 16
DH = D // H
F = 1024
KT = D // P
QT = S // P
NT = B * QT
FT = F // P
CT = B * SC
G = 4
NG = H // G
UB = QT * NG
SCALE = 1.0 / 16.0
MASK = -1e10
EPS = 1e-6
TERMS = [(0, 0), (0, 1), (0, 2), (1, 0), (1, 1), (2, 0)]
NTERM = len(TERMS)
KS = NTERM * DH
CB = 6
CCH = [(c * SC, min(CB, B - c) * SC) for c in range(0, B, CB)]
SCE = SC + 1


def f32(ap):
    return ap.bitcast(F32)


def dyn(ap, i, n=1):
    if isinstance(i, int):
        return ap[i] if n == 1 else ap[i:i + n]
    v = ap[bass.ds(i, n)]
    return v.squeeze(0) if n == 1 else v


def dyn1(ap, i, n):
    return ap[:, i:i + n] if isinstance(i, int) else ap[:, bass.ds(i, n)]


def pairs(eng, body, tail=False):
    for u in range(2):
        body(0, u)
    with eng.Fori(1, B // 2) as j:
        for u in range(2):
            body(j, u)
    if tail:
        body(B // 2, 0)


def atleast(eng, s, v):
    if not (isinstance(v, int) and v <= 0):
        eng.wait_ge(s, v)


class Sems:

    def __init__(self, nc):
        self.nc, self.held, self.n = nc, [], 0

    def stage(self, fn, *args, **kw):
        made = fn(self.nc, *args, **kw)
        self.nc.clear_and_free_semaphores(self.held)
        self.nc.all_engine_barrier()
        self.held = []
        return made

    def __call__(self, name):
        self.n += 1
        self.held.append(self.nc.alloc_semaphore(f"{name}_{self.n}"))
        return self.held[-1]


def mm3(pe, out, a, b, kts, start=True, stop=True):
    last = None
    seq = [(kt, x, y) for kt in kts for x, y in ((0, 0), (1, 0), (0, 1))]
    for n, (kt, x, y) in enumerate(seq):
        last = pe.matmul(out, a(x, kt), b(y, kt), start=start and n == 0, stop=stop and n == len(seq) - 1)
    return last


def setup_constants(nc, sem, t):
    zeroed, made = sem("const_zeroed"), sem("const_made")
    with nc.Block() as block:
        @block.gpsimd
        def _(pool):
            nc.gpsimd.memset(t.ident[:], 0.0).then_inc(zeroed, 1)
            nc.gpsimd.memset(t.identb[:], 0.0).then_inc(zeroed, 1)
            nc.gpsimd.memset(t.maskb[:], 0.0).then_inc(zeroed, 1)
            pool.wait_ge(zeroed, 3)
            for m in (t.ident, t.identb):
                nc.gpsimd.affine_select(out=m[:], in_=m[:], compare_op=ALU.not_equal, fill=1.0, base=0,
                                        pattern=[[-1, P]], channel_multiplier=1).then_inc(made, 1)
            nc.gpsimd.affine_select(out=t.maskb[:], in_=t.maskb[:], compare_op=ALU.is_ge, fill=MASK, base=0,
                                    pattern=[[0, G], [-1, P]], channel_multiplier=1).then_inc(made, 1)


def split_weights(nc, ctx, sem, jobs):
    loaded = [sem("w_loaded") for _ in range(2)]
    high_done, low_done = sem("w_high"), sem("w_low")
    cols = max(j[1].shape[1] * j[1].shape[2] for j in jobs)
    stage = ctx.enter_context(nc.sbuf_tensor(f"wstage{sem.n}", [P, 2, cols], F32))

    def view(n):
        kt, c = jobs[n][1].shape[1], jobs[n][1].shape[2]
        return stage[:, n % 2, 0:kt * c].rearrange("p (k c) -> p k c", k=kt)

    with nc.Block() as block:
        @block.sync
        def _(sp):
            for n, (w, hi, lo, s) in enumerate(jobs):
                if n >= 2:
                    sp.wait_ge(low_done, n - 1)
                sp.dma_start(view(n), w.rearrange("(k p) c -> p k c", p=P)).then_inc(loaded[n % 2], 16)

        @block.scalar
        def _(act):
            for n, (w, hi, lo, s) in enumerate(jobs):
                act.wait_ge(loaded[n % 2], 16 * (n // 2 + 1))
                nc.scalar.activation(hi, view(n), ACT.Copy, scale=s).then_inc(high_done, 1)

        @block.vector
        def _(dve):
            for n, (w, hi, lo, s) in enumerate(jobs):
                dve.wait_ge(high_done, n + 1)
                nc.vector.scalar_tensor_tensor(lo, view(n), s, f32(hi), ALU.mult, ALU.subtract).then_inc(low_done, 1)


def split_context(nc, ctx, sem, ctxT, ch, cl):
    split_weights(nc, ctx, sem, [(ctxT, ch[:], cl[:], 1.0)])


def context_kv(nc, ctx, sem, t, wk, wv, kparts_dram):
    parts = ctx.enter_context(nc.sbuf_tensor("ckparts", [P, KT, 3, CT], BF16))
    rest = ctx.enter_context(nc.sbuf_tensor("ckrest", [P, CT], F32))
    pk = [ctx.enter_context(nc.psum_tensor(f"ck{i}", [P, 512], F32)) for i in range(3)]
    pv = [ctx.enter_context(nc.psum_tensor(f"cv{i}", [P, 512], F32)) for i in range(2)]
    k_ready, p1, r1, p2, p3 = sem("ck_ready"), sem("ck_p1"), sem("ck_r1"), sem("ck_p2"), sem("ck_p3")
    v_ready, v_used, stored = sem("cv_ready"), sem("cv_used"), sem("ck_stored")
    nc3 = len(CCH)
    ch, cl = t.ch, t.cl
    with nc.Block() as block:
        @block.tensor
        def _(pe):
            for ot in range(KT):
                for c, (c0, cn) in enumerate(CCH):
                    if ot:
                        pe.wait_ge(r1, c + 1)
                    mm3(nc.tensor, pk[c][:, 0:cn], lambda x, kt: wk[x][:, kt, ot * P:(ot + 1) * P],
                        lambda y, kt: (ch, cl)[y][:, kt, c0:c0 + cn], range(KT)).then_inc(k_ready, 1)
            for b in range(B):
                if b >= 2:
                    pe.wait_ge(v_used, b - 1)
                mm3(nc.tensor, pv[b % 2][0:SC, 0:D], lambda x, kt: (ch, cl)[x][:, kt, b * SC:(b + 1) * SC],
                    lambda y, kt: wv[y][:, kt, :], range(KT)).then_inc(v_ready, 1)

        @block.scalar
        def _(act):
            for n in range(KT * nc3):
                ot, c = divmod(n, nc3)
                c0, cn = CCH[c]
                act.wait_ge(k_ready, n + 1)
                nc.scalar.activation(parts[:, ot, 0, c0:c0 + cn], pk[c][:, 0:cn], ACT.Copy).then_inc(p1, 1)
                act.wait_ge(r1, n + 1)
                nc.scalar.activation(parts[:, ot, 1, c0:c0 + cn], rest[:, c0:c0 + cn], ACT.Copy).then_inc(p2, 1)

        @block.vector
        def _(dve):
            for n in range(KT * nc3):
                ot, c = divmod(n, nc3)
                c0, cn = CCH[c]
                dve.wait_ge(p1, n + 1)
                if ot:
                    dve.wait_ge(p3, n + 1 - nc3)
                nc.vector.tensor_tensor(rest[:, c0:c0 + cn], pk[c][:, 0:cn], parts[:, ot, 0, c0:c0 + cn],
                                        ALU.subtract).then_inc(r1, 1)
                dve.wait_ge(p2, n + 1)
                nc.vector.tensor_tensor(parts[:, ot, 2, c0:c0 + cn], rest[:, c0:c0 + cn],
                                        parts[:, ot, 1, c0:c0 + cn], ALU.subtract).then_inc(p3, 1)
            for b in range(B):
                dve.wait_ge(v_ready, b + 1)
                nc.vector.tensor_copy(t.vc[:, b, :], pv[b % 2][0:SC, 0:D]).then_inc(v_used, 1)

        @block.sync
        def _(sp):
            sp.wait_ge(p3, KT * nc3)
            sp.dma_start(kparts_dram.rearrange("k p c -> p k c"),
                         parts[:].rearrange("p k t c -> p k (t c)")).then_inc(stored, 16)
            sp.wait_ge(stored, 16)


def project(nc, ctx, sem, t, src, weights, parts_dram, wv=None, ln=None):
    nw = len(weights)
    wcols = nw * S
    sb = lambda n, s, d: ctx.enter_context(nc.sbuf_tensor(n + str(sem.n), s, d))
    ps = lambda n: ctx.enter_context(nc.psum_tensor(n + str(sem.n), [P, 512], F32))
    xh = [sb(f"xh{u}", [P, KT, S], F32R) for u in range(2)]
    xl = [sb(f"xl{u}", [P, KT, S], F32R) for u in range(2)]
    parts = [sb(f"parts{u}", [P, KT, 3, wcols], BF16) for u in range(2)]
    rest = sb("rest", [P, KT, wcols], F32)
    qk = [[ps(f"qk{u}{ot}") for ot in range(KT)] for u in range(2)]
    if ln is None:
        raw = [sb(f"raw{u}", [P, KT, S], F32) for u in range(2)]
        vps = [ps(f"vps{u}") for u in range(2)]
        loaded = [sem("x_loaded") for _ in range(2)]
    x_high, x_low = sem("x_high"), sem("x_low")
    qk_ready, v_ready, v_used = sem("qk_ready"), sem("v_ready"), sem("v_used")
    part1, remainder, part2, part3 = sem("part1"), sem("remainder"), sem("part2"), sem("part3")
    stored = [sem("parts_stored") for _ in range(2)]
    if ln is not None:
        hT = ln_tiles(nc, ctx, sem, t, ln)

    with nc.Block() as block:
        @block.sync
        def _(sp):
            def body(j, u):
                b = 2 * j + u
                if ln is None:
                    atleast(sp, x_low, b - 1)
                    sp.dma_start(raw[u][:], dyn(src, b)).then_inc(loaded[u], 16)
            pairs(sp, body) if ln is None else None

        @block.gpsimd
        def _(pool):
            def store(b, j, u):
                pool.wait_ge(part3, KT * b + KT)
                pool.dma_start(dyn(parts_dram, b), parts[u][:].rearrange("p k t c -> p k (t c)")).then_inc(stored[u], 16)

            if ln is not None:
                def body(j, u):
                    hT.copy_back(pool, j, u)
                    store(2 * j + u, j, u)
            else:
                def body(j, u):
                    store(2 * j + u, j, u)
            pairs(pool, body)
            for u in range(2):
                pool.wait_ge(stored[u], 16 * (B // 2))

        @block.scalar
        def _(act):
            def body(j, u):
                b = 2 * j + u
                if ln is None:
                    act.wait_ge(loaded[u], 16 * (j + 1))
                    x = raw[u][:]
                else:
                    act.wait_ge(hT.turned, b + 1)
                    x = hT.ps[u][:, :].rearrange("p (k s) -> p k s", k=KT)
                atleast(act, v_ready if wv else qk_ready, (b - 1) if wv else KT * (b - 1))
                nc.scalar.activation(xh[u][:], x, ACT.Copy).then_inc(x_high, 1)
                for ot in range(KT):
                    n = KT * b + ot
                    act.wait_ge(qk_ready, n + 1)
                    atleast(act, stored[u], 16 * j)
                    nc.scalar.activation(parts[u][:, ot, 0, :], qk[u][ot][:, 0:wcols], ACT.Copy).then_inc(part1, 1)
                    act.wait_ge(remainder, n + 1)
                    nc.scalar.activation(parts[u][:, ot, 1, :], rest[:, ot, :], ACT.Copy).then_inc(part2, 1)
            pairs(act, body)

        @block.vector
        def _(dve):
            def body(j, u):
                b = 2 * j + u
                if ln is None:
                    x = raw[u][:]
                else:
                    hT.normalise(dve, j, u)
                    x = hT.ps[u][:, :].rearrange("p (k s) -> p k s", k=KT)
                dve.wait_ge(x_high, b + 1)
                nc.vector.tensor_tensor(xl[u][:], x, f32(xh[u][:]), ALU.subtract).then_inc(x_low, 1)
                for ot in range(KT):
                    n = KT * b + ot
                    dve.wait_ge(part1, n + 1)
                    atleast(dve, part3, n + 1 - KT)
                    nc.vector.tensor_tensor(rest[:, ot, :], qk[u][ot][:, 0:wcols], parts[u][:, ot, 0, :],
                                            ALU.subtract).then_inc(remainder, 1)
                    dve.wait_ge(part2, n + 1)
                    nc.vector.tensor_tensor(parts[u][:, ot, 2, :], rest[:, ot, :], parts[u][:, ot, 1, :],
                                            ALU.subtract).then_inc(part3, 1)
                if wv:
                    dve.wait_ge(v_ready, b + 1)
                    nc.vector.tensor_copy(dyn1(t.vs, QT * b, QT), vps[u][:, :].rearrange("p (q d) -> p q d", q=QT)).then_inc(v_used, 1)
            pairs(dve, body)

        @block.tensor
        def _(pe):
            def body(j, u):
                b = 2 * j + u
                if ln is not None:
                    hT.turn(pe, j, u)
                pe.wait_ge(x_low, b + 1)
                for ot in range(KT):
                    atleast(pe, remainder, KT * (b - 2) + ot + 1)
                    for w, wt in enumerate(weights):
                        last = mm3(nc.tensor, qk[u][ot][:, w * S:(w + 1) * S],
                                   lambda x, kt: wt[x][:, kt, ot * P:(ot + 1) * P],
                                   lambda y, kt: (xh, xl)[y][u][:, kt, :], range(KT))
                    last.then_inc(qk_ready, 1)
                if wv:
                    atleast(pe, v_used, b - 1)
                    for qt in range(QT):
                        last = mm3(nc.tensor, vps[u][:, qt * D:(qt + 1) * D],
                                   lambda x, kt: (xh, xl)[x][u][:, kt, qt * P:(qt + 1) * P],
                                   lambda y, kt: wv[y][:, kt, :], range(KT))
                    last.then_inc(v_ready, 1)
            pairs(pe, body)


class ln_tiles:

    def __init__(self, nc, ctx, sem, t, ln):
        sb = lambda n, s, d: ctx.enter_context(nc.sbuf_tensor(n + str(sem.n), s, d))
        self.nc, self.t = nc, t
        self.gamma, self.beta = ln
        self.cent = [sb(f"cent{u}", [P, QT, D], F32) for u in range(2)]
        self.h = [sb(f"h{u}", [P, QT, D], F32) for u in range(2)]
        self.ps = [ctx.enter_context(nc.psum_tensor(f"hT{u}{sem.n}", [P, 512], F32)) for u in range(2)]
        self.centred, self.normed, self.copied = sem("centred"), sem("normed"), sem("copied_back")
        self.turned, self.evacuated = sem("turned"), None

    def normalise(self, dve, j, u):
        b = 2 * j + u
        t = self.t
        for qt in range(QT):
            n = QT * b + qt
            atleast(dve, self.normed, QT * (b - 2) + qt + 1)
            r = dyn1(t.res, n, 1)[:, 0, :]
            mean = dyn1(t.mean, n, 1)
            self.nc.vector.scalar_tensor_tensor(self.cent[u][:, qt, :], r, mean, self.gamma, ALU.subtract,
                                                ALU.mult).then_inc(self.centred, 1)
            dve.wait_ge(self.centred, n + 1)
            atleast(dve, self.copied, b - 1)
            atleast(dve, self.turned, b - 1)
            self.nc.vector.scalar_tensor_tensor(self.h[u][:, qt, :], self.cent[u][:, qt, :], dyn1(t.rstd, n, 1),
                                                self.beta, ALU.mult, ALU.add).then_inc(self.normed, 1)

    def copy_back(self, pool, j, u):
        b = 2 * j + u
        pool.wait_ge(self.normed, QT * b + QT)
        pool.nop(nofuse=True)
        self.nc.gpsimd.tensor_copy(dyn1(self.t.res, QT * b, QT), self.h[u][:]).then_inc(self.copied, 1)

    def turn(self, pe, j, u, freed=None):
        b = 2 * j + u
        pe.wait_ge(self.normed, QT * b + QT)
        for kt in range(KT):
            for qt in range(QT):
                last = self.nc.tensor.transpose(self.ps[u][:, kt * S + qt * P:kt * S + (qt + 1) * P],
                                                self.h[u][:, qt, kt * P:(kt + 1) * P], self.t.ident[:])
        last.then_inc(self.turned, 1)


def attention(nc, ctx, sem, t, causal, wo, load_stacks, n_loads, v_all, x_dram):
    nk = P if causal else SC
    sb = lambda n, s, d: ctx.enter_context(nc.sbuf_tensor(n + str(sem.n), s, d))
    ps = lambda n, c: ctx.enter_context(nc.psum_tensor(n + str(sem.n), [P, c], F32))
    skeys = S if causal else SC
    KV = QT if causal else 1
    s_vpad = sem("v_spread")
    sq = [sb(f"sq{u}", [KS, H, S], BF16) for u in range(2)]
    sk = [sb(f"sk{u}", [KS, H, skeys], BF16) for u in range(2)]
    prob = [sb(f"prob{i}", [P, G * (S if causal else SC)], F32) for i in range(4)]
    negmax = [sb(f"negmax{i}", [P, G], F32) for i in range(4)]
    sums = [sb(f"sums{i}", [P, G], F32) for i in range(4)]
    recip = [sb(f"recip{i}", [P, G], F32) for i in range(4)]
    probT = [sb(f"probT{i}", [P, G, P], F32) for i in range(4)]
    vpad = [sb(f"vpad{i}", [P, KV, H, 2 * DH], F32) for i in range(2)]
    zeroed = sem("vpad_zeroed")
    oh = [sb(f"oh{i}", [P, KT, P], F32R) for i in range(QT)]
    ol = [sb(f"ol{i}", [P, KT, P], F32R) for i in range(QT)]
    stat = sb("stat", [P, 6], F32)
    agg = sb("agg", [P, 2], F32)
    rstat = sb("rstat", [P, QT, D], F32)
    s_mv, s_keep = sem("mv_ready"), sem("res_kept")
    score = [ps(f"score{i}", 1024) for i in range(2)]
    turn = [ps(f"turn{i}", 512) for i in range(2)]
    oy = [ps(f"oy{i}", 512) for i in range(QT)]
    if causal:
        xt = [sb(f"xt{i}", [P, QT, D], F32) for i in range(2)]
        x_loaded = [sem("xt_loaded") for _ in range(2)]
    stacked = [sem("stacked") for _ in range(2)]
    s_score, s_max, s_exp, s_recip, s_norm = sem("score_ready"), sem("max_ready"), sem("exp_ready"), sem("recip_ready"), sem("norm_ready")
    s_turn, s_evac, s_av = sem("probT_ready"), sem("probT_copied"), sem("av_ready")
    s_oh, s_ol, s_y, s_res, s_stat, s_agg = sem("o_high"), sem("o_low"), sem("y_ready"), sem("res_ready"), sem("stat_ready"), sem("agg_ready")

    def halves(u):
        return u // NG + 1 if causal else 1

    HB = sum(halves(u) for u in range(UB))

    def half0(u):
        return sum(halves(v) for v in range(u))

    def steps(eng, step, lag):
        for k in range(2):
            for u in range(UB):
                step(k, u, k)
        with eng.Fori(1, B // 2) as j:
            for k in range(2):
                for u in range(UB):
                    step(2 * j + k, u, k)
        for u in range(lag):
            step(B, u, 0)

    def back(b, u, k, lag):
        v, kk = u, k
        while lag:
            lag -= 1
            v -= 1
            if v < 0:
                v, b, kk = UB - 1, b - 1, 1 - kk
        if isinstance(b, int) and b < 0:
            return None
        return b, v, kk

    with nc.Block() as block:
        @block.sync
        def _(sp):
            def body(j, k):
                b = 2 * j + k
                atleast(sp, s_score, UB * (b - 1))
                load_stacks(sp, b, sq[k], sk[k], stacked[k])
                if causal:
                    atleast(sp, s_res, QT * (b - 1))
                    sp.dma_start(xt[k][:], dyn(x_dram, b)).then_inc(x_loaded[k], 16)
            pairs(sp, body)

        @block.tensor
        def _(pe):
            mt = nc.tensor.matmul

            def scores(b, u, k):
                if isinstance(b, int) and b >= B:
                    return
                qt, g = divmod(u, NG)
                if u == 0:
                    pe.wait_ge(stacked[k], 16 * n_loads * ((b - k) // 2 + 1) if isinstance(b, int) else 8 * n_loads * (b - k) + 16 * n_loads)
                atleast(pe, s_exp, UB * b + u - 1)
                ps_ = score[u % 2]
                w = nk * halves(u) if causal else SC
                if causal:
                    if qt == 0:
                        mt(ps_[:, 0:G * P], t.identb[:], t.maskb[:].rearrange("p g k -> p (g k)"), start=True, stop=False, skip_group_check=True)
                    else:
                        for bank in range(2):
                            mt(ps_[:, bank * 512:(bank + 1) * 512].rearrange("p (h k) -> p h k", h=2)[:, :, P:S],
                               t.identb[:], t.maskb[:, 0:2, :], start=True, stop=False, skip_group_check=True)
                for h in range(G):
                    last = mt(ps_[:, h * w:(h + 1) * w], sq[k][:, G * g + h, qt * P:(qt + 1) * P],
                              sk[k][:, G * g + h, 0:w], start=not causal, stop=True, skip_group_check=True)
                last.then_inc(s_score, 1)

            def transposes(b, u, k):
                pe.wait_ge(s_norm, UB * b + u + 1)
                w = nk * halves(u)
                for kt in range(halves(u)):
                    n = HB * b + half0(u) + kt
                    slot = (half0(u) + kt) % 2
                    atleast(pe, s_evac, n - 1)
                    for h in range(G):
                        last = nc.tensor.transpose(turn[slot][0:nk, h * P:(h + 1) * P],
                                                   prob[u % 4][:, h * w + kt * nk:h * w + (kt + 1) * nk], t.ident[:])
                    last.then_inc(s_turn, 1)

            def av(b, u, k):
                qt, g = divmod(u, NG)
                if g == 0:
                    atleast(pe, s_res, QT * (b - 1) + qt + 1)
                if u == 0:
                    pe.wait_ge(s_vpad, 2 * KV * (b + 1))
                pe.wait_ge(s_evac, HB * b + half0(u) + halves(u))
                for hp in range(0, G, 2):
                    q = 32 * ((G * g + hp) % (P // DH) // 2)
                    tile = G * g // (P // DH)
                    seq = [(h, kt) for h in (hp, hp + 1) for kt in range(halves(u))]
                    for i, (h, kt) in enumerate(seq):
                        last = mt(oy[qt][q:q + 32, tile * P:(tile + 1) * P], vpad[k][0:nk, kt, G * g + h, :],
                                  probT[(half0(u) + kt) % 4][0:nk, h, :], start=i == 0, stop=i == len(seq) - 1,
                                  skip_group_check=True)
                last.then_inc(s_av, 1)

            def project_out(b, u, k):
                qt, g = divmod(u, NG)
                if g == NG - 1:
                    pe.wait_ge(s_ol, QT * b + qt + 1)
                    mm3(nc.tensor, oy[qt][:, D:2 * D], lambda x, kt: (oh, ol)[x][qt][:, kt, :],
                        lambda y, kt: wo[y][:, kt, :], range(KT)).then_inc(s_y, 1)

            def step(b, u, k):
                scores(b, u, k)
                for fn, lag in ((transposes, 2), (project_out, 4), (av, 3)):
                    at = back(b, u, k, lag)
                    if at is not None and not (isinstance(at[0], int) and at[0] >= B):
                        fn(*at)
            steps(pe, step, 4)

        @block.scalar
        def _(act):
            def exps(b, u, k):
                w = nk * halves(u)
                act.wait_ge(s_max, UB * b + u + 1)
                atleast(act, s_turn, HB * b + half0(u) - sum(halves((u - 1 - i) % UB) for i in range(3)))
                atleast(act, s_recip, UB * b + u - 3)
                for h in range(G):
                    last = nc.scalar.activation(prob[u % 4][:, h * w:(h + 1) * w], score[u % 2][:, h * w:(h + 1) * w],
                                                ACT.Exp, bias=negmax[u % 4][:, h:h + 1], accum_out=sums[u % 4][:, h:h + 1])
                last.then_inc(s_exp, 1)

            def high(b, u, k):
                qt, g = divmod(u, NG)
                if g == NG - 1:
                    act.wait_ge(s_av, UB * b + u + 1)
                    atleast(act, s_y, QT * (b - 1) + qt + 1)
                    nc.scalar.activation(oh[qt][:], oy[qt][:, 0:D].rearrange("p (k q) -> p k q", k=KT),
                                         ACT.Copy).then_inc(s_oh, 1)

            def keep(b, u, k):
                qt, g = divmod(u, NG)
                if g == NG - 1:
                    n = QT * b + qt
                    act.wait_ge(s_res, n + 1)
                    nc.scalar.activation(dyn1(t.res, n, 1)[:, 0, :], rstat[:, qt, :], ACT.Copy).then_inc(s_keep, 1)

            def step(b, u, k):
                if not (isinstance(b, int) and b >= B):
                    exps(b, u, k)
                for fn, lag in ((high, 3), (keep, 5)):
                    at = back(b, u, k, lag)
                    if at is not None and not (isinstance(at[0], int) and at[0] >= B):
                        fn(*at)
            steps(act, step, 5)

        @block.gpsimd
        def _(pool):
            for v in vpad:
                nc.gpsimd.memset(v[:], 0.0).then_inc(zeroed, 1)
            pool.wait_ge(zeroed, 2)

            def step(b, u, k):
                w = nk * halves(u)
                if u == 0:
                    atleast(pool, s_av, UB * (b - 1))
                    pool.nop(nofuse=True)
                    for e in range(2):
                        for kt in range(KV):
                            src = dyn1(v_all, KV * b + kt, 1)[:, 0, :].rearrange("p (m e d) -> p m e d", e=2, d=DH)[:, :, e, :]
                            dst = vpad[k][0:nk, kt, :, :].rearrange("p (m e) c -> p m e c", e=2)[:, :, e, e * DH:(e + 1) * DH]
                            nc.gpsimd.tensor_copy(dst, src).then_inc(s_vpad, 1)
                pool.wait_ge(s_recip, UB * b + u + 1)
                v = prob[u % 4][:, 0:G * w].rearrange("p (h k) -> p h k", h=G)
                nc.gpsimd.tensor_tensor(v, v, recip[u % 4][:].unsqueeze(2).broadcast_to([P, G, w]),
                                        ALU.mult).then_inc(s_norm, 1)
            steps(pool, step, 0)

        @block.vector
        def _(dve):
            def maxes(b, u, k):
                w = nk * halves(u)
                dve.wait_ge(s_score, UB * b + u + 1)
                atleast(dve, s_exp, UB * b + u - 3)
                nc.vector.tensor_reduce(negmax[u % 4][:], score[u % 2][:, 0:G * w].rearrange("p (h k) -> p h k", h=G),
                                        AX.X, ALU.max, negate=True).then_inc(s_max, 1)

            def recips(b, u, k):
                dve.wait_ge(s_exp, UB * b + u + 1)
                atleast(dve, s_norm, UB * b + u - 3)
                nc.vector.reciprocal(recip[u % 4][:], sums[u % 4][:]).then_inc(s_recip, 1)

            def evac(b, u, k):
                for kt in range(halves(u)):
                    n = HB * b + half0(u) + kt
                    dve.wait_ge(s_turn, n + 1)
                    v = (half0(u) + kt) % HB
                    m = (v - 4) % HB
                    m_unit = max(x for x in range(UB) if half0(x) <= m)
                    atleast(dve, s_av, UB * (b if v >= 4 else b - 1) + m_unit + 1)
                    nc.vector.tensor_copy(probT[v % 4][0:nk, :, :],
                                          turn[v % 2][0:nk, :].rearrange("p (h q) -> p h q", h=G)).then_inc(s_evac, 1)

            def low(b, u, k):
                qt, g = divmod(u, NG)
                if g == NG - 1:
                    dve.wait_ge(s_oh, QT * b + qt + 1)
                    nc.vector.tensor_tensor(ol[qt][:], oy[qt][:, 0:D].rearrange("p (k q) -> p k q", k=KT),
                                            f32(oh[qt][:]), ALU.subtract).then_inc(s_ol, 1)

            def residual(b, u, k):
                qt, g = divmod(u, NG)
                if g == NG - 1:
                    n = QT * b + qt
                    dve.wait_ge(s_y, n + 1)
                    r = dyn1(t.res, n, 1)[:, 0, :]
                    if causal:
                        dve.wait_ge(x_loaded[k], 16 * (b // 2 + 1) if isinstance(b, int) else 8 * (b - k) + 16)
                    atleast(dve, s_keep, QT * (b - 1) + qt + 1)
                    nc.vector.tensor_tensor(rstat[:, qt, :], oy[qt][:, D:2 * D], xt[k][:, qt, :] if causal else r,
                                            ALU.add).then_inc(s_res, 1)
                    statistics(nc, dve, t, n, rstat[:, qt, :], stat, agg, s_res, s_stat, s_agg, s_mv)

            def step(b, u, k):
                if not (isinstance(b, int) and b >= B):
                    maxes(b, u, k)
                for fn, lag in ((recips, 1), (evac, 2), (low, 3), (residual, 4)):
                    at = back(b, u, k, lag)
                    if at is not None and not (isinstance(at[0], int) and at[0] >= B):
                        fn(*at)
            steps(dve, step, 4)


def statistics(nc, dve, t, n, r, stat, agg, s_res, s_stat, s_agg, s_mv):
    dve.wait_ge(s_res, n + 1)
    atleast(dve, s_agg, n)
    nc.vector.bn_stats(stat[:], r).then_inc(s_stat, 1)
    dve.wait_ge(s_stat, n + 1)
    atleast(dve, s_mv, n)
    dve.nop(nofuse=True)
    nc.vector.bn_aggr(agg[:], stat[:]).then_inc(s_agg, 1)
    dve.wait_ge(s_agg, n + 1)
    nc.vector.tensor_copy(dyn1(t.mv, n, 1)[:, 0, :], agg[:]).then_inc(s_mv, 1)


def finish_stats(nc, sem, t):
    mean_done, std_done, eps_done, done = sem("mean"), sem("std"), sem("std_eps"), sem("rstd")
    with nc.Block() as block:
        @block.scalar
        def _(act):
            nc.scalar.activation(t.std[:], t.mv[:, :, 1], ACT.Sqrt, scale=D / (D - 1.0)).then_inc(std_done, 1)

        @block.vector
        def _(dve):
            nc.vector.tensor_copy(t.mean[:], t.mv[:, :, 0]).then_inc(mean_done, 1)
            dve.wait_ge(std_done, 1)
            nc.vector.tensor_scalar(t.rstd[:], t.std[:], EPS, None, ALU.add).then_inc(eps_done, 1)
            dve.wait_ge(eps_done, 1)
            nc.vector.reciprocal(t.rstd[:], t.rstd[:]).then_inc(done, 1)


def feed_forward(nc, ctx, sem, t, w1, w2, b1, b2, ln):
    sb = lambda n, s, d: ctx.enter_context(nc.sbuf_tensor(n + str(sem.n), s, d))
    ps = lambda n: ctx.enter_context(nc.psum_tensor(n + str(sem.n), [P, 512], F32))
    hT = ln_tiles(nc, ctx, sem, t, ln)
    xh = [sb(f"fxh{u}", [P, KT, S], F32R) for u in range(2)]
    xl = [sb(f"fxl{u}", [P, KT, S], F32R) for u in range(2)]
    hid = [sb(f"hid{u}", [P, S], F32) for u in range(2)]
    hh = [sb(f"hh{u}", [P, FT, S], F32R) for u in range(2)]
    hl = [sb(f"hl{u}", [P, FT, S], F32R) for u in range(2)]
    part = sb("ffpart", [P, D], F32)
    stat = sb("ffstat", [P, 6], F32)
    agg = sb("ffagg", [P, 2], F32)
    rstat = sb("ffrstat", [P, QT, D], F32)
    s_mv, s_keep = sem("ff_mv"), sem("ff_kept")
    up = [ps(f"up{i}") for i in range(2)]
    down = [ps(f"down{i}") for i in range(QT)]
    s_xh, s_xl, s_up, s_hid, s_hh, s_hl = sem("ff_xh"), sem("ff_xl"), sem("up_ready"), sem("hid_ready"), sem("hid_high"), sem("hid_low")
    s_down, s_part, s_res, s_stat, s_agg = sem("down_ready"), sem("ff_part"), sem("ff_res"), sem("ff_stat"), sem("ff_agg")

    with nc.Block() as block:
        @block.tensor
        def _(pe):
            def down_step(j, u):
                b = 2 * j + u
                for qt in range(QT):
                    atleast(pe, s_res, QT * (b - 1) + qt + 1)
                    pe.wait_ge(s_hl, FT * b + FT)
                    mm3(nc.tensor, down[qt][:, 0:D], lambda x, m: (hh, hl)[x][u][:, m, qt * P:(qt + 1) * P],
                        lambda y, m: w2[y][:, m, :], range(FT)).then_inc(s_down, 1)

            def body(j, u, more=True):
                b = 2 * j + u
                pe.wait_ge(s_xl, b + 1)
                for m in range(FT):
                    n = FT * b + m
                    atleast(pe, s_hid, n - 1)
                    mm3(nc.tensor, up[m % 2][:, 0:S], lambda x, kt: w1[x][:, kt, m * P:(m + 1) * P],
                        lambda y, kt: (xh, xl)[y][u][:, kt, :], range(KT)).then_inc(s_up, 1)
                    if m == FT // 2 - 1 and more:
                        hT.turn(pe, *((j + 1, 0) if u else (j, 1)))
                if not (isinstance(j, int) and j == 0 and u == 0):
                    down_step(*((j, 0) if u else (j - 1, 1)))

            hT.turn(pe, 0, 0)
            for u in range(2):
                body(0, u)
            with pe.Fori(1, B // 2 - 1) as j:
                for u in range(2):
                    body(j, u)
            body(B // 2 - 1, 0)
            body(B // 2 - 1, 1, False)
            down_step(B // 2 - 1, 1)

        @block.scalar
        def _(act):
            def body(j, u):
                b = 2 * j + u
                act.wait_ge(hT.turned, b + 1)
                atleast(act, s_up, FT * (b - 1))
                nc.scalar.activation(xh[u][:], hT.ps[u][:, :].rearrange("p (k s) -> p k s", k=KT), ACT.Copy).then_inc(s_xh, 1)
                for m in range(FT):
                    n = FT * b + m
                    act.wait_ge(s_up, n + 1)
                    atleast(act, s_hl, n - 1)
                    nc.scalar.activation(hid[m % 2][:], up[m % 2][:, 0:S], ACT.Relu, bias=b1[:, m:m + 1]).then_inc(s_hid, 1)
                    if m == FT // 2 and not (isinstance(j, int) and j == 0 and u == 0):
                        keep(*((j, 0) if u else (j - 1, 1)), late=1)

            def keep(j, u, late=0):
                for qt in range(QT):
                    n = QT * (2 * j + u) + qt
                    if late:
                        n = n - QT
                        if isinstance(n, int) and n < 0:
                            continue
                    act.wait_ge(s_res, n + 1)
                    nc.scalar.activation(dyn1(t.res, n, 1)[:, 0, :], rstat[:, qt, :], ACT.Copy).then_inc(s_keep, 1)
            pairs(act, body)
            keep(B // 2 - 1, 0)
            keep(B // 2 - 1, 1)

        @block.gpsimd
        def _(pool):
            def body(j, u):
                b = 2 * j + u
                hT.copy_back(pool, j, u)
                for m in range(FT):
                    n = FT * b + m
                    pool.wait_ge(s_hid, n + 1)
                    if m == 0:
                        atleast(pool, s_down, QT * (b - 1))
                    pool.nop(nofuse=True)
                    nc.gpsimd.tensor_copy(hh[u][:, m, :], hid[m % 2][:]).then_inc(s_hh, 1)
            pairs(pool, body)

        @block.vector
        def _(dve):
            def finish(j, u):
                b = 2 * j + u
                for qt in range(QT):
                    n = QT * b + qt
                    r = dyn1(t.res, n, 1)[:, 0, :]
                    dve.wait_ge(s_down, n + 1)
                    dve.wait_ge(hT.copied, b + 1)
                    atleast(dve, s_res, n)
                    nc.vector.tensor_tensor(part[:], down[qt][:, 0:D], b2[:], ALU.add).then_inc(s_part, 1)
                    dve.wait_ge(s_part, n + 1)
                    atleast(dve, s_keep, QT * (b - 1) + qt + 1)
                    nc.vector.tensor_tensor(rstat[:, qt, :], part[:], r, ALU.add).then_inc(s_res, 1)
                    statistics(nc, dve, t, n, rstat[:, qt, :], stat, agg, s_res, s_stat, s_agg, s_mv)

            def low(j, u):
                b = 2 * j + u
                dve.wait_ge(s_xh, b + 1)
                nc.vector.tensor_tensor(xl[u][:], hT.ps[u][:, :].rearrange("p (k s) -> p k s", k=KT),
                                        f32(xh[u][:]), ALU.subtract).then_inc(s_xl, 1)

            def hidden(j, u, ms):
                for m in ms:
                    n = FT * (2 * j + u) + m
                    dve.wait_ge(s_hh, n + 1)
                    nc.vector.tensor_tensor(hl[u][:, m, :], hid[m % 2][:], f32(hh[u][:, m, :]), ALU.subtract).then_inc(s_hl, 1)

            def body(j, u, more=True):
                hidden(j, u, range(0, 2))
                if more:
                    normalise(j, 1) if u == 0 else normalise(j + 1, 0)
                hidden(j, u, range(2, 4))
                hidden(j, u, range(4, FT))
                if not (isinstance(j, int) and j == 0 and u == 0):
                    finish(*((j, 0) if u else (j - 1, 1)))
                if more:
                    low(j, 1) if u == 0 else low(j + 1, 0)

            def normalise(j, u):
                hT.normalise(dve, j, u)

            hT.normalise(dve, 0, 0)
            low(0, 0)
            for u in range(2):
                body(0, u)
            with dve.Fori(1, B // 2 - 1) as j:
                for u in range(2):
                    body(j, u)
            body(B // 2 - 1, 0)
            body(B // 2 - 1, 1, False)
            finish(B // 2 - 1, 1)


def replicate_column(nc, ctx, sem, col, rep):
    zero = ctx.enter_context(nc.sbuf_tensor("zeros", [P, P], F32))
    full = ctx.enter_context(nc.sbuf_tensor("rep_full", [P, KT, P], F32))
    zeroed, filled, rounded, split = (sem(n) for n in ("zeroed", "filled", "rounded", "rep_split"))
    with nc.Block() as block:
        @block.vector
        def _(dve):
            nc.vector.memset(zero[:], 0.0).then_inc(zeroed, 1)
            dve.wait_ge(zeroed, 1)
            for kt in range(KT):
                nc.vector.tensor_scalar(full[:, kt, :], zero[:], col[:, kt:kt + 1], None, ALU.add).then_inc(filled, 1)
            dve.wait_ge(filled, KT)
            nc.vector.tensor_copy(rep[0][:], full[:]).then_inc(rounded, 1)
            dve.wait_ge(rounded, 1)
            nc.vector.tensor_tensor(rep[1][:], full[:], f32(rep[0][:]), ALU.subtract).then_inc(split, 1)


class Job:

    def __init__(self, rows, cols, stat, mov, full=None, halves=None, scale=1.0, col=None, row=None, after=0):
        self.rows, self.cols, self.stat, self.mov, self.full, self.halves = rows, cols, stat, mov, full, halves
        self.scale, self.col, self.row, self.after = scale, col, row, after


def product_jobs(nc, ctx, sem, jobs):
    ps = [ctx.enter_context(nc.psum_tensor(f"job{i}_{sem.n}", [P, 512], F32)) for i in range(2)]
    stage = [ctx.enter_context(nc.sbuf_tensor(f"jobf{i}_{sem.n}", [P, 512], F32)) for i in range(2)]
    made, moved, high, low = (sem(n) for n in ("job_made", "job_moved", "job_high", "job_low"))
    split = [0]
    for job in jobs:
        split.append(split[-1] + (job.halves is not None))

    def shaped(v, o):
        return v if len(o.shape) == 2 else v.rearrange("p (b k) -> p b k", k=SC)

    def staged(n):
        job = jobs[n]
        return job.full if job.full is not None else stage[n % 2][0:job.rows, 0:job.cols]

    with nc.Block() as block:
        @block.tensor
        def _(pe):
            for n, job in enumerate(jobs):
                if n >= 2:
                    pe.wait_ge(moved, n - 1)
                if job.after:
                    pe.wait_ge(low, split[job.after])
                mm3(nc.tensor, ps[n % 2][0:job.rows, 0:job.cols], job.stat, job.mov, range(KT)).then_inc(made, 1)

        @block.vector
        def _(dve):
            for n, job in enumerate(jobs):
                dve.wait_ge(made, n + 1)
                if split[max(n - 1, 0)]:
                    dve.wait_ge(low, split[n - 1])
                src = ps[n % 2][0:job.rows, 0:job.cols]
                if job.row is not None:
                    nc.vector.tensor_tensor(staged(n), src, job.row, ALU.add).then_inc(moved, 1)
                elif job.col is not None:
                    nc.vector.tensor_scalar(staged(n), src, job.col, None, ALU.add).then_inc(moved, 1)
                else:
                    nc.vector.tensor_scalar(staged(n), src, job.scale, None, ALU.mult).then_inc(moved, 1)
                if job.halves is not None:
                    hi, lo = job.halves
                    dve.wait_ge(high, split[n + 1])
                    nc.vector.tensor_tensor(lo, shaped(staged(n), lo), f32(hi), ALU.subtract).then_inc(low, 1)

        @block.scalar
        def _(act):
            for n, job in enumerate(jobs):
                if job.halves is not None:
                    hi = job.halves[0]
                    act.wait_ge(moved, n + 1)
                    nc.scalar.activation(hi, shaped(staged(n), hi), ACT.Copy).then_inc(high, 1)


def gated_prep_scores(nc, ctx, sem, t, g):
    c, jobs = (t.ch, t.cl), []
    for ot in range(KT):
        o = slice(ot * P, (ot + 1) * P)
        for c0, cn in CCH:
            jobs.append(Job(P, cn, lambda x, kt, o=o: g.wk[x][:, kt, o], lambda y, kt, c0=c0, cn=cn: c[y][:, kt, c0:c0 + cn],
                            halves=[k[:, ot, c0:c0 + cn] for k in g.kp], col=g.bk[:, ot:ot + 1]))
    n_kp = len(jobs)
    kp = lambda c0, cn: lambda y, kt: g.kp[y][:, kt, c0:c0 + cn]
    rep = lambda x, kt: g.rep[x][:, kt, :]
    for ot in range(KT):
        o = slice(ot * P, (ot + 1) * P)
        for c0, cn in CCH:
            jobs.append(Job(P, cn, lambda x, kt, o=o: g.wqT[x][:, kt, o], kp(c0, cn), scale=SCALE, after=n_kp,
                            halves=[v[:, ot, c0 // SC:(c0 + cn) // SC, 0:SC] for v in g.a]))
        jobs.append(Job(P, D, lambda x, kt, o=o: g.wqT[x][:, kt, o], lambda y, kt: g.wg1[y][:, kt, :],
                        halves=[v[:, ot, :] for v in g.wqg]))
    for c0, cn in CCH:
        jobs.append(Job(P, cn, rep, kp(c0, cn), scale=SCALE, full=g.cb[:, c0:c0 + cn]))
    jobs.append(Job(P, D, rep, lambda y, kt: g.wg1[y][:, kt, :], full=g.gb[:], row=g.bg[:]))
    product_jobs(nc, ctx, sem, jobs)


def gated_prep_values(nc, ctx, sem, t, g):
    c, jobs = (t.ch, t.cl), []
    for ot in range(KT):
        o = slice(ot * P, (ot + 1) * P)
        for c0, cn in CCH:
            jobs.append(Job(P, cn, lambda x, kt, o=o: g.wv[x][:, kt, o], lambda y, kt, c0=c0, cn=cn: c[y][:, kt, c0:c0 + cn],
                            halves=[k[:, ot, c0:c0 + cn] for k in g.vpT], col=g.bv[:, ot:ot + 1]))
    n_vp = len(jobs)
    for b in range(B):
        k = slice(b * SC, (b + 1) * SC)
        jobs.append(Job(SC, D, lambda x, kt, k=k: c[x][:, kt, k], lambda y, kt: g.wv[y][:, kt, :], row=g.bvr[0:SC, :],
                        halves=[v[:, b, 0:D] for v in g.vv]))
        jobs.append(Job(SC, D, lambda x, kt, k=k: g.vpT[x][:, kt, k], lambda y, kt: g.wg2[y][:, kt, :], after=n_vp,
                        halves=[v[:, b, D:2 * D] for v in g.vv]))
    product_jobs(nc, ctx, sem, jobs)


def gated_attention(nc, ctx, sem, t, g, ln, mask, out):
    sb = lambda n, s, d: ctx.enter_context(nc.sbuf_tensor(n + str(sem.n), s, d))
    ps = lambda n: ctx.enter_context(nc.psum_tensor(n + str(sem.n), [P, 512], F32))
    hT = ln_tiles(nc, ctx, sem, t, ln)
    xh = [sb(f"gxh{u}", [P, KT, S], F32R) for u in range(2)]
    xl = [sb(f"gxl{u}", [P, KT, S], F32R) for u in range(2)]
    s_sb, p_sb = sb("gs", [P, QT, SC], F32), [sb(f"gp{u}", [P, QT, SC], F32) for u in range(2)]
    nmax, sums, rec = sb("gnm", [P, QT], F32), sb("gsum", [P, QT], F32), sb("grec", [P, QT], F32)
    pth, ptl = sb("gpth", [SC, QT, P], F32R), sb("gptl", [SC, QT, P], F32R)
    gq_sb = [sb(f"ggq{u}", [P, QT, D], F32) for u in range(2)]
    gate, sig, sig1, gated = (sb(n, [P, QT, D], F32) for n in ("gate", "gsig", "gsig1", "gated"))
    fin = [sb(f"fin{u}", [P, QT, D], F32) for u in range(2)]
    sc, gq, pt = ps("gsc"), ps("ggqp"), ps("gpt")
    xo = [ps(f"gxo{q}") for q in range(QT)]
    names = ("g_xh", "g_xl", "g_sc", "g_s", "g_max", "g_gq", "g_gqb", "g_exp", "g_rec", "g_p", "g_pt", "g_pth", "g_ptl",
             "g_xo", "g_gate", "g_sig", "g_sig1", "g_inv", "g_gated", "g_fin")
    (s_xh, s_xl, s_sc, s_s, s_max, s_gq, s_gqb, s_exp, s_rec, s_p, s_pt, s_pth, s_ptl, s_xo, s_gate, s_sig, s_sig1,
     s_inv, s_gated, s_fin) = (sem(n) for n in names)
    stored = [sem("out_stored") for _ in range(2)]

    def run(eng, front, later, back, ahead=None):
        def step(j, u, f=True, bk=True, a=True):
            prev = (j, 0) if u else (j - 1, 1)
            nxt = (j + 1, 0) if u else (j, 1)
            for kind, fn in front:
                at = {"now": (j, u), "prev": prev, "next": nxt}[kind]
                if {"now": f, "prev": bk, "next": a}[kind]:
                    fn(*at)
        step(0, 0, bk=False)
        step(0, 1)
        with eng.Fori(1, B // 2 - 1) as j:
            for u in range(2):
                step(j, u)
        step(B // 2 - 1, 0)
        step(B // 2 - 1, 1, a=False)
        step(B // 2, 0, f=False, a=False)

    with nc.Block() as block:
        @block.tensor
        def _(pe):
            def turn_p(j, u):
                b = 2 * j + u
                pe.wait_ge(s_p, QT * (b + 1))
                atleast(pe, s_ptl, b)
                for q in range(QT):
                    last = nc.tensor.transpose(pt[0:SC, q * P:(q + 1) * P], p_sb[u][:, q, :], t.ident[:])
                last.then_inc(s_pt, 1)

            def scores(j, u):
                b = 2 * j + u
                pe.wait_ge(s_xl, b + 1)
                atleast(pe, s_s, b)
                for q in range(QT):
                    last = mm3(nc.tensor, sc[:, q * SCE:(q + 1) * SCE], lambda x, kt: (xh, xl)[x][u][:, kt, q * P:(q + 1) * P],
                               lambda y, kt: dyn1(g.a[y][:, kt, :, :], b, 1)[:, 0, :], range(KT))
                last.then_inc(s_sc, 1)

            def gates(j, u):
                b = 2 * j + u
                atleast(pe, s_gqb, b)
                for q in range(QT):
                    last = mm3(nc.tensor, gq[:, q * D:(q + 1) * D], lambda x, kt: (xh, xl)[x][u][:, kt, q * P:(q + 1) * P],
                               lambda y, kt: g.wqg[y][:, kt, :], range(KT))
                last.then_inc(s_gq, 1)

            def mix(j, u):
                b = 2 * j + u
                pe.wait_ge(s_ptl, b + 1)
                atleast(pe, s_gated, QT * b)
                for q in range(QT):
                    mm3(nc.tensor, xo[q][:], lambda x, kt: (pth, ptl)[x][:, q, :],
                        lambda y, kt: dyn1(g.vv[y], b, 1)[:, 0, :], range(1)).then_inc(s_xo, 1)

            hT.turn(pe, 0, 0)
            run(pe, [("prev", turn_p), ("now", scores), ("now", gates), ("prev", mix), ("next", lambda j, u: hT.turn(pe, j, u))], None, None)

        @block.scalar
        def _(act):
            def high(j, u):
                act.wait_ge(hT.turned, 2 * j + u + 1)
                atleast(act, s_gq, 2 * j + u - 1)
                nc.scalar.activation(xh[u][:], hT.ps[u][:, :].rearrange("p (k s) -> p k s", k=KT), ACT.Copy).then_inc(s_xh, 1)

            def p_high(j, u):
                b = 2 * j + u
                act.wait_ge(s_pt, b + 1)
                atleast(act, s_xo, QT * b)
                nc.scalar.activation(pth[:], pt[0:SC, 0:S].rearrange("p (q s) -> p q s", q=QT), ACT.Copy).then_inc(s_pth, 1)

            def exps(j, u):
                b = 2 * j + u
                act.wait_ge(s_max, b + 1)
                atleast(act, s_pt, b - 1)
                atleast(act, s_rec, b)
                for q in range(QT):
                    last = nc.scalar.activation(p_sb[u][:, q, :], s_sb[:, q, :], ACT.Exp, bias=nmax[:, q:q + 1],
                                                accum_out=sums[:, q:q + 1])
                last.then_inc(s_exp, 1)

            def sigmoid(j, u):
                b = 2 * j + u
                act.wait_ge(s_gate, QT * (b + 1))
                atleast(act, s_sig1, b)
                nc.scalar.activation(sig[:], gate[:], ACT.Exp, scale=-1.0).then_inc(s_sig, 1)

            high(0, 0)
            run(act, [("prev", p_high), ("now", exps), ("prev", sigmoid), ("next", high)], None, None)

        @block.vector
        def _(dve):
            def low(j, u):
                dve.wait_ge(s_xh, 2 * j + u + 1)
                nc.vector.tensor_tensor(xl[u][:], hT.ps[u][:, :].rearrange("p (k s) -> p k s", k=KT), f32(xh[u][:]),
                                        ALU.subtract).then_inc(s_xl, 1)

            def p_low(j, u):
                dve.wait_ge(s_pth, 2 * j + u + 1)
                nc.vector.tensor_tensor(ptl[:], pt[0:SC, 0:S].rearrange("p (q s) -> p q s", q=QT), f32(pth[:]),
                                        ALU.subtract).then_inc(s_ptl, 1)

            def shifted(j, u):
                b = 2 * j + u
                dve.wait_ge(s_sc, b + 1)
                atleast(dve, s_exp, b)
                nc.vector.tensor_tensor(s_sb[:], sc[:, 0:QT * SCE].rearrange("p (q k) -> p q k", q=QT)[:, :, 0:SC],
                                        dyn1(g.cb[:].rearrange("p (b k) -> p b k", k=SC), b, 1).broadcast_to([P, QT, SC]),
                                        ALU.add).then_inc(s_s, 1)
                dve.wait_ge(s_s, b + 1)
                nc.vector.tensor_reduce(nmax[:], s_sb[:], AX.X, ALU.max, negate=True).then_inc(s_max, 1)

            def gate_q(j, u):
                b = 2 * j + u
                dve.wait_ge(s_gq, b + 1)
                atleast(dve, s_gate, QT * (b - 1))
                nc.vector.tensor_tensor(gq_sb[u][:], gq[:].rearrange("p (q d) -> p q d", q=QT),
                                        g.gb[:].unsqueeze(1).broadcast_to([P, QT, D]), ALU.add).then_inc(s_gqb, 1)

            def scale_p(j, u):
                b = 2 * j + u
                dve.wait_ge(s_exp, b + 1)
                nc.vector.reciprocal(rec[:], sums[:]).then_inc(s_rec, 1)
                dve.wait_ge(s_rec, b + 1)
                for q in range(QT):
                    nc.vector.tensor_scalar(p_sb[u][:, q, :], p_sb[u][:, q, :], rec[:, q:q + 1], None, ALU.mult).then_inc(s_p, 1)

            def gate_sum(j, u):
                b = 2 * j + u
                for q in range(QT):
                    dve.wait_ge(s_xo, QT * b + q + 1)
                    atleast(dve, s_sig, b)
                    nc.vector.tensor_tensor(gate[:, q, :], xo[q][:, D:2 * D], gq_sb[u][:, q, :], ALU.add).then_inc(s_gate, 1)

            def finish(j, u):
                b = 2 * j + u
                dve.wait_ge(s_sig, b + 1)
                nc.vector.tensor_scalar(sig1[:], sig[:], 1.0, None, ALU.add).then_inc(s_sig1, 1)
                dve.wait_ge(s_sig1, b + 1)
                nc.vector.reciprocal(sig1[:], sig1[:]).then_inc(s_inv, 1)
                dve.wait_ge(s_inv, b + 1)
                atleast(dve, s_fin, b)
                for q in range(QT):
                    nc.vector.scalar_tensor_tensor(gated[:, q, :], xo[q][:, 0:D], dyn1(mask[:], QT * b + q, 1), sig1[:, q, :],
                                                   ALU.mult, ALU.mult).then_inc(s_gated, 1)

            hT.normalise(dve, 0, 0)
            low(0, 0)
            run(dve, [("prev", p_low), ("now", shifted), ("now", gate_q), ("next", lambda j, u: hT.normalise(dve, j, u)),
                      ("now", scale_p), ("prev", gate_sum), ("prev", finish), ("next", low)], None, None)

        @block.gpsimd
        def _(pool):
            def add(j, u):
                b = 2 * j + u
                pool.wait_ge(s_gated, QT * (b + 1))
                pool.wait_ge(hT.copied, b + 1)
                atleast(pool, stored[u], 16 * j)
                nc.gpsimd.tensor_tensor(fin[u][:], gated[:], dyn1(t.res, QT * b, QT), ALU.add).then_inc(s_fin, 1)

            hT.copy_back(pool, 0, 0)
            run(pool, [("next", lambda j, u: hT.copy_back(pool, j, u)), ("prev", add)], None, None)

        @block.sync
        def _(sp):
            def body(j, u):
                b = 2 * j + u
                sp.wait_ge(s_fin, b + 1)
                sp.dma_start(dyn(out, b), fin[u][:]).then_inc(stored[u], 16)
            pairs(sp, body)
            for u in range(2):
                sp.wait_ge(stored[u], 16 * (B // 2))


class Tensors:
    pass


def program(nc, a, out):
    with ExitStack() as whole:
        sem = Sems(nc)
        run = sem.stage

        def sb(name, shape, dt, ctx=whole):
            return ctx.enter_context(nc.sbuf_tensor(name, shape, dt))

        t = Tensors()
        t.ident, t.identb = sb("ident", [P, P], F32), sb("identb", [P, P], BF16)
        t.maskb = sb("maskb", [P, G, P], BF16)
        t.res = sb("res", [P, NT, D], F32)
        t.mv, t.mean, t.std, t.rstd = sb("mv", [P, NT, 2], F32), sb("mean", [P, NT], F32), sb("std", [P, NT], F32), sb("rstd", [P, NT], F32)
        t.ch, t.cl = sb("ctx_high", [P, KT, CT], F32R), sb("ctx_low", [P, KT, CT], F32R)
        rows = {n: sb(n, [P, D], F32) for n in ("ln1_g", "ln1_b", "ln2_g", "ln2_b", "ln3_g", "ln3_b", "ff_b2", "bg", "bvr")}
        cols = {n: sb(n + "_col", [P, k], F32) for n, k in (("ff_b1", FT), ("bq", KT), ("bk", KT), ("bv", KT))}
        mask = sb("mask", [P, NT], F32)
        qk_dram = nc.dram_tensor("qk_parts", (B, KT, P, 3 * 2 * S), BF16).ap()
        q_dram = nc.dram_tensor("q_parts", (B, KT, P, 3 * S), BF16).ap()
        kc_dram = nc.dram_tensor("kc_parts", (KT, P, 3 * CT), BF16).ap()
        run(setup_constants, sem, t)

        small = whole.enter_context(nc.semaphore("small_loaded"))
        with nc.Block() as block:
            @block.sync
            def _(sp):
                n = 0
                src = dict(bg="L1_xattn_bg", bvr="L1_xattn_bv")
                for k, v in rows.items():
                    sp.dma_start(v[:], a[src.get(k, "L0_xattn_" + k)].partition_broadcast(P)).then_inc(small, 16)
                    n += 1
                for k, v in cols.items():
                    w = a[k + "_col"]
                    sp.dma_start(v[:], w).then_inc(small, 16)
                    n += 1
                sp.dma_start(mask[:], a["maskT"]).then_inc(small, 16)
                sp.wait_ge(small, 16 * (n + 1))

        def weights(ctx, names, kts, colsn):
            jobs, out_ = [], []
            for (name, ap, scale), kt, c in zip(names, kts, colsn):
                w = [sb(f"{name}{i}", [P, kt, c], F32R, ctx) for i in range(2)]
                jobs.append((ap, w[0][:], w[1][:], scale))
                out_.append(w)
            with ExitStack() as st:
                run(split_weights, st, sem, jobs)
            return out_

        def stacks(parts, qcol, width, kparts):
            def load(sp, b, sq, sk, s):
                for term, (pq, pk) in enumerate(TERMS):
                    rows_ = slice(term * DH, (term + 1) * DH)
                    v = dyn(parts, b).rearrange("k (m d) (t w s) -> t w d (k m) s", d=DH, t=3, s=S)
                    sp.dma_start(sq[rows_, :, :], v[pq, 0]).then_inc(s, 16)
                    if kparts is None:
                        sp.dma_start(sk[rows_, :, :], v[pk, 1]).then_inc(s, 16)
                    else:
                        kv = kparts.rearrange("k (m d) (t b s) -> b t d (k m) s", d=DH, t=3, s=SC)
                        sp.dma_start(sk[rows_, :, :], dyn(kv, b)[pk]).then_inc(s, 16)
            return load

        A = lambda n: a["L0_xattn_" + n]
        context = ExitStack()
        t.vc = sb("vc", [SC, B, D], F32, context)
        with ExitStack() as ctx:
            wk, wv = weights(ctx, [("cwk", A("ca_wk"), 1.0), ("cwv", A("ca_wv"), 1.0)], [KT] * 2, [D] * 2)
            with ExitStack() as st:
                run(split_context, st, sem, a["ctxT"], t.ch, t.cl)
            run(context_kv, ctx, sem, t, wk, wv, kc_dram)

        with ExitStack() as sa:
            t.vs = sb("vs", [P, NT, D], F32, sa)
            wo, = weights(sa, [("swo", A("sa_wo"), 1.0)], [KT], [D])
            with ExitStack() as ctx:
                wq, wk, wv = weights(ctx, [("swq", A("sa_wq"), SCALE), ("swk", A("sa_wk"), 1.0), ("swv", A("sa_wv"), 1.0)],
                                     [KT] * 3, [D] * 3)
                run(project, ctx, sem, t, a["xT"].rearrange("b (k p) s -> b p k s", p=P), [wq, wk],
                        qk_dram.rearrange("b k p c -> b p k c"), wv=wv)
            with ExitStack() as ctx:
                run(attention, ctx, sem, t, True, wo, stacks(qk_dram, 0, 2, None), 2 * NTERM, t.vs,
                          a["x"].rearrange("b (q p) d -> b p q d", p=P))
        run(finish_stats, sem, t)

        with ExitStack() as ca:
            wo, = weights(ca, [("cwo", A("ca_wo"), 1.0)], [KT], [D])
            with ExitStack() as ctx:
                wq, = weights(ctx, [("cwq", A("ca_wq"), SCALE)], [KT], [D])
                run(project, ctx, sem, t, None, [wq], q_dram.rearrange("b k p c -> b p k c"),
                        ln=(rows["ln1_g"][:], rows["ln1_b"][:]))
            with ExitStack() as ctx:
                run(attention, ctx, sem, t, False, wo, stacks(q_dram, 0, 1, kc_dram), 2 * NTERM, t.vc, None)
        context.close()
        run(finish_stats, sem, t)

        with ExitStack() as ctx:
            w1, w2 = weights(ctx, [("fw1", A("ff_w1"), 1.0), ("fw2", A("ff_w2"), 1.0)], [KT, FT], [F, D])
            run(feed_forward, ctx, sem, t, w1, w2, cols["ff_b1"], rows["ff_b2"], (rows["ln2_g"][:], rows["ln2_b"][:]))
        run(finish_stats, sem, t)

        with ExitStack() as ctx:
            g = Tensors()
            g.a = [sb(f"ga{i}", [P, KT, B, SCE], F32R, ctx) for i in range(2)]
            g.wqg = [sb(f"gwqg{i}", [P, KT, D], F32R, ctx) for i in range(2)]
            g.cb, g.gb = sb("gcb", [P, CT], F32, ctx), sb("ggb", [P, D], F32, ctx)
            g.bq, g.bk, g.bv, g.bg, g.bvr = cols["bq"], cols["bk"], cols["bv"], rows["bg"], rows["bvr"]
            spare = ctx.enter_context(nc.semaphore("spare_column"))
            with nc.Block() as block:
                @block.vector
                def _(dve):
                    for v in g.a:
                        nc.vector.memset(f32(v[:, :, :, SC:SCE]), 0.0).then_inc(spare, 1)
            with ExitStack() as st:
                g.kp = [sb(f"gkp{i}", [P, KT, CT], F32R, st) for i in range(2)]
                g.rep = [sb(f"bq_rep{i}", [P, KT, P], F32R, st) for i in range(2)]
                g.wqT, g.wk, g.wg1 = weights(st, [("gwqT", a["WqT"], 1.0), ("gwk", a["L1_xattn_Wk"], 1.0),
                                                  ("gwg1", a["L1_xattn_Wg"][0:D, :], 1.0)], [KT] * 3, [D] * 3)
                run(replicate_column, st, sem, g.bq, g.rep)
                run(gated_prep_scores, st, sem, t, g)
            g.vv = [sb(f"gvv{i}", [SC, B, 2 * D], F32R, ctx) for i in range(2)]
            with ExitStack() as st:
                g.vpT = [sb(f"gvpT{i}", [P, KT, CT], F32R, st) for i in range(2)]
                g.wv, g.wg2 = weights(st, [("gwv", a["L1_xattn_Wv"], 1.0), ("gwg2", a["L1_xattn_Wg"][D:2 * D, :], 1.0)],
                                      [KT] * 2, [D] * 2)
                run(gated_prep_values, st, sem, t, g)
            run(gated_attention, ctx, sem, t, g, (rows["ln3_g"][:], rows["ln3_b"][:]), mask,
                            out.rearrange("b (q p) d -> b p q d", p=P))


def kernel(**inputs):
    import numpy as np
    import concourse.bacc as bacc
    from concourse.bass_utils import run_bass_kernel_spmd

    nc = bacc.Bacc("TRN2", target_bir_lowering=False, num_devices=1)
    laid = {n: np.ascontiguousarray(v) for n, v in inputs.items()}
    laid["xT"] = np.ascontiguousarray(laid["x"].transpose(0, 2, 1))
    laid["ctxT"] = np.ascontiguousarray(laid.pop("ctx_1024").reshape(CT, D).T)
    laid["WqT"] = np.ascontiguousarray(laid.pop("L1_xattn_Wq").T)
    for n in ("sa_wq", "sa_wk", "sa_wv", "sa_wo", "ca_wq", "ca_wk", "ca_wv", "ca_wo", "ff_w1", "ff_w2"):
        laid["L0_xattn_" + n] = np.ascontiguousarray(laid["L0_xattn_" + n].T)
    laid["maskT"] = np.ascontiguousarray(laid.pop("mask_BxS_ff1").reshape(NT, P).T)
    for k, n in (("ff_b1", "L0_xattn_ff_b1"), ("bq", "L1_xattn_bq"), ("bk", "L1_xattn_bk"), ("bv", "L1_xattn_bv")):
        laid[k + "_col"] = np.ascontiguousarray(laid[n].reshape(-1, P).T)
    arrays, aps = {}, {}
    for n, v in laid.items():
        arrays["in_" + n] = v
        aps[n] = nc.dram_tensor("in_" + n, v.shape, mybir.dt.from_np(v.dtype), kind="ExternalInput").ap()
    out = nc.dram_tensor("out", (B, S, D), F32, kind="ExternalOutput").ap()
    program(nc, aps, out)
    return run_bass_kernel_spmd(nc, [arrays], core_ids=[0]).results[0]["out"]
```

```python
from contextlib import ExitStack

import concourse.bass as bass
from concourse import mybir

F32 = mybir.dt.float32
F32R = mybir.dt.float32r
BF16 = mybir.dt.bfloat16
ACT = mybir.ActivationFunctionType
ALU = mybir.AluOpType
AX = mybir.AxisListType

P = 128
B = 16
S = 256
SC = 77
D = 256
H = 16
DH = D // H
F = 1024
KT = D // P
QT = S // P
NT = B * QT
FT = F // P
CT = B * SC
G = 4
SCALE = 1.0 / 16.0
MASK = -1e10
EPS = 1e-6
TERMS = [(0, 0), (0, 1), (0, 2), (1, 0), (1, 1), (2, 0)]
NTERM = len(TERMS)
KS = NTERM * DH
CB = 6
CCH = [(c * SC, min(CB, B - c) * SC) for c in range(0, B, CB)]
SCE = SC + 1


def f32(ap):
    return ap.bitcast(F32)


def dyn(ap, i, n=1):
    if isinstance(i, int):
        return ap[i] if n == 1 else ap[i:i + n]
    v = ap[bass.ds(i, n)]
    return v.squeeze(0) if n == 1 else v


def dyn1(ap, i, n):
    return ap[:, i:i + n] if isinstance(i, int) else ap[:, bass.ds(i, n)]


def pairs(eng, body):
    for u in range(2):
        body(0, u)
    with eng.Fori(1, B // 2) as j:
        for u in range(2):
            body(j, u)


def skewed(eng, items):
    ahead, behind = max([0] + [-lag for lag, _ in items]), max([0] + [lag for lag, _ in items])
    start, end = max(1, (behind + 1) // 2), (B - ahead) // 2

    def step(j, u):
        for lag, fn in items:
            c, v = j + (u - lag) // 2, (u - lag) % 2
            if not isinstance(c, int) or 0 <= 2 * c + v < B:
                fn(c, v)

    for n in range(-ahead, 2 * start):
        step(n // 2, n % 2)
    with eng.Fori(start, end) as j:
        step(j, 0)
        step(j, 1)
    for n in range(2 * end, B + behind):
        step(n // 2, n % 2)


def atleast(eng, s, v):
    if not (isinstance(v, int) and v <= 0):
        eng.wait_ge(s, v)


class Sems:

    def __init__(self, nc):
        self.nc, self.held, self.n = nc, [], 0

    def stage(self, fn, *args, **kw):
        made = fn(self.nc, *args, **kw)
        self.nc.clear_and_free_semaphores(self.held)
        self.nc.all_engine_barrier()
        self.held = []
        return made

    def __call__(self, name):
        self.n += 1
        self.held.append(self.nc.alloc_semaphore(f"{name}_{self.n}"))
        return self.held[-1]


def mm3(pe, out, a, b, kts, start=True, stop=True):
    last = None
    seq = [(kt, x, y) for kt in kts for x, y in ((0, 0), (1, 0), (0, 1))]
    for n, (kt, x, y) in enumerate(seq):
        last = pe.matmul(out, a(x, kt), b(y, kt), start=start and n == 0, stop=stop and n == len(seq) - 1)
    return last


def setup_constants(nc, sem, t):
    zeroed, made = sem("const_zeroed"), sem("const_made")
    with nc.Block() as block:
        @block.gpsimd
        def _(pool):
            nc.gpsimd.memset(t.ident[:], 0.0).then_inc(zeroed, 1)
            nc.gpsimd.memset(t.identb[:], 0.0).then_inc(zeroed, 1)
            nc.gpsimd.memset(t.maskb[:], 0.0).then_inc(zeroed, 1)
            pool.wait_ge(zeroed, 3)
            for m in (t.ident, t.identb):
                nc.gpsimd.affine_select(out=m[:], in_=m[:], compare_op=ALU.not_equal, fill=1.0, base=0,
                                        pattern=[[-1, P]], channel_multiplier=1).then_inc(made, 1)
            nc.gpsimd.affine_select(out=t.maskb[:], in_=t.maskb[:], compare_op=ALU.is_ge, fill=MASK, base=0,
                                    pattern=[[0, G], [-1, P]], channel_multiplier=1).then_inc(made, 1)


def split_weights(nc, ctx, sem, jobs):
    loaded = [sem("w_loaded") for _ in range(2)]
    high_done, low_done = sem("w_high"), sem("w_low")
    cols = max(j[1].shape[1] * j[1].shape[2] for j in jobs)
    stage = ctx.enter_context(nc.sbuf_tensor(f"wstage{sem.n}", [P, 2, cols], F32))

    def view(n):
        kt, c = jobs[n][1].shape[1], jobs[n][1].shape[2]
        return stage[:, n % 2, 0:kt * c].rearrange("p (k c) -> p k c", k=kt)

    with nc.Block() as block:
        @block.sync
        def _(sp):
            for n, (w, hi, lo, s) in enumerate(jobs):
                if n >= 2:
                    sp.wait_ge(low_done, n - 1)
                sp.dma_start(view(n), w.rearrange("(k p) c -> p k c", p=P)).then_inc(loaded[n % 2], 16)

        @block.scalar
        def _(act):
            for n, (w, hi, lo, s) in enumerate(jobs):
                act.wait_ge(loaded[n % 2], 16 * (n // 2 + 1))
                nc.scalar.activation(hi, view(n), ACT.Copy, scale=s).then_inc(high_done, 1)

        @block.vector
        def _(dve):
            for n, (w, hi, lo, s) in enumerate(jobs):
                dve.wait_ge(high_done, n + 1)
                nc.vector.scalar_tensor_tensor(lo, view(n), s, f32(hi), ALU.mult, ALU.subtract).then_inc(low_done, 1)


def split_context(nc, ctx, sem, ctxT, ch, cl):
    split_weights(nc, ctx, sem, [(ctxT, ch[:], cl[:], 1.0)])


def context_kv(nc, ctx, sem, t, wk, wv, kparts_dram):
    parts = ctx.enter_context(nc.sbuf_tensor("ckparts", [P, KT, 3, CT], BF16))
    rest = ctx.enter_context(nc.sbuf_tensor("ckrest", [P, CT], F32))
    pk = [ctx.enter_context(nc.psum_tensor(f"ck{i}", [P, 512], F32)) for i in range(3)]
    pv = [ctx.enter_context(nc.psum_tensor(f"cv{i}", [P, 512], F32)) for i in range(2)]
    k_ready, p1, r1, p2, p3 = sem("ck_ready"), sem("ck_p1"), sem("ck_r1"), sem("ck_p2"), sem("ck_p3")
    v_ready, v_used, stored = sem("cv_ready"), sem("cv_used"), sem("ck_stored")
    nc3 = len(CCH)
    ch, cl = t.ch, t.cl
    with nc.Block() as block:
        @block.tensor
        def _(pe):
            for ot in range(KT):
                for c, (c0, cn) in enumerate(CCH):
                    if ot:
                        pe.wait_ge(r1, c + 1)
                    mm3(nc.tensor, pk[c][:, 0:cn], lambda x, kt: wk[x][:, kt, ot * P:(ot + 1) * P],
                        lambda y, kt: (ch, cl)[y][:, kt, c0:c0 + cn], range(KT)).then_inc(k_ready, 1)
            for b in range(B):
                if b >= 2:
                    pe.wait_ge(v_used, b - 1)
                mm3(nc.tensor, pv[b % 2][0:SC, 0:D], lambda x, kt: (ch, cl)[x][:, kt, b * SC:(b + 1) * SC],
                    lambda y, kt: wv[y][:, kt, :], range(KT)).then_inc(v_ready, 1)

        @block.scalar
        def _(act):
            for n in range(KT * nc3):
                ot, c = divmod(n, nc3)
                c0, cn = CCH[c]
                act.wait_ge(k_ready, n + 1)
                nc.scalar.activation(parts[:, ot, 0, c0:c0 + cn], pk[c][:, 0:cn], ACT.Copy).then_inc(p1, 1)
                act.wait_ge(r1, n + 1)
                nc.scalar.activation(parts[:, ot, 1, c0:c0 + cn], rest[:, c0:c0 + cn], ACT.Copy).then_inc(p2, 1)

        @block.vector
        def _(dve):
            for n in range(KT * nc3):
                ot, c = divmod(n, nc3)
                c0, cn = CCH[c]
                dve.wait_ge(p1, n + 1)
                if ot:
                    dve.wait_ge(p3, n + 1 - nc3)
                nc.vector.tensor_tensor(rest[:, c0:c0 + cn], pk[c][:, 0:cn], parts[:, ot, 0, c0:c0 + cn],
                                        ALU.subtract).then_inc(r1, 1)
                dve.wait_ge(p2, n + 1)
                nc.vector.tensor_tensor(parts[:, ot, 2, c0:c0 + cn], rest[:, c0:c0 + cn],
                                        parts[:, ot, 1, c0:c0 + cn], ALU.subtract).then_inc(p3, 1)
            for b in range(B):
                dve.wait_ge(v_ready, b + 1)
                nc.vector.tensor_copy(t.vc[:, b, :], pv[b % 2][0:SC, 0:D]).then_inc(v_used, 1)

        @block.sync
        def _(sp):
            sp.wait_ge(p3, KT * nc3)
            sp.dma_start(kparts_dram.rearrange("k p c -> p k c"),
                         parts[:].rearrange("p k t c -> p k (t c)")).then_inc(stored, 16)
            sp.wait_ge(stored, 16)


def project(nc, ctx, sem, t, src, weights, parts_dram, wv=None, ln=None):
    nw = len(weights)
    wcols = nw * S
    sb = lambda n, s, d: ctx.enter_context(nc.sbuf_tensor(n + str(sem.n), s, d))
    ps = lambda n, c: ctx.enter_context(nc.psum_tensor(n + str(sem.n), [P, c], F32))
    xh = [sb(f"xh{u}", [P, KT, S], F32R) for u in range(2)]
    xl = [sb(f"xl{u}", [P, KT, S], F32R) for u in range(2)]
    parts = [sb(f"parts{u}", [P, KT, 3, wcols], BF16) for u in range(2)]
    rest = sb("rest", [P, KT, wcols], F32)
    qk = [ps(f"qk{u}", KT * wcols) for u in range(2)]
    qk3 = [v[:].rearrange("p (k c) -> p k c", k=KT) for v in qk]
    if ln is None:
        raw = [sb(f"raw{u}", [P, KT, S], F32) for u in range(2)]
        vps = [ps(f"vps{u}", QT * D) for u in range(2)]
        loaded = [sem("x_loaded") for _ in range(2)]
        x = [raw[u][:] for u in range(2)]
    else:
        hT = ln_tiles(nc, ctx, sem, t, ln)
        x = [hT.ps[u][:].rearrange("p (k s) -> p k s", k=KT) for u in range(2)]
    x_high, x_low = sem("x_high"), sem("x_low")
    qk_ready, v_ready, v_used = sem("qk_ready"), sem("v_ready"), sem("v_used")
    part1, remainder, part2, part3 = sem("part1"), sem("remainder"), sem("part2"), sem("part3")
    stored = [sem("parts_stored") for _ in range(2)]

    with nc.Block() as block:
        @block.sync
        def _(sp):
            def load(j, u):
                atleast(sp, x_low, 2 * j + u - 1)
                sp.dma_start(raw[u][:], dyn(src, 2 * j + u)).then_inc(loaded[u], 16)

            def store(j, u):
                sp.wait_ge(part3, 2 * j + u + 1)
                sp.dma_start(dyn(parts_dram, 2 * j + u), parts[u][:].rearrange("p k t c -> p k (t c)")).then_inc(stored[u], 16)

            skewed(sp, [(-1, load)] if ln is None else [(1, store)])
            for u in range(2):
                sp.wait_ge(stored[u], 16 * (B // 2))

        @block.gpsimd
        def _(pool):
            def store(j, u):
                pool.wait_ge(part3, 2 * j + u + 1)
                pool.dma_start(dyn(parts_dram, 2 * j + u), parts[u][:].rearrange("p k t c -> p k (t c)")).then_inc(stored[u], 16)

            skewed(pool, [(-2, lambda j, u: hT.copy_back(pool, j, u))] if ln is not None else [(1, store)])

        @block.scalar
        def _(act):
            def high(j, u):
                b = 2 * j + u
                if ln is None:
                    act.wait_ge(loaded[u], 16 * (j + 1))
                else:
                    act.wait_ge(hT.turned, b + 1)
                atleast(act, v_ready if wv else qk_ready, b - 1)
                nc.scalar.activation(xh[u][:], x[u], ACT.Copy).then_inc(x_high, 1)

            def first(j, u):
                b = 2 * j + u
                act.wait_ge(qk_ready, b + 1)
                atleast(act, stored[u], 16 * j)
                nc.scalar.activation(parts[u][:, :, 0, :], qk3[u], ACT.Copy).then_inc(part1, 1)

            def second(j, u):
                act.wait_ge(remainder, 2 * j + u + 1)
                nc.scalar.activation(parts[u][:, :, 1, :], rest[:], ACT.Copy).then_inc(part2, 1)

            skewed(act, [(1, first), (-1, high), (1, second)])

        @block.vector
        def _(dve):
            def low(j, u):
                dve.wait_ge(x_high, 2 * j + u + 1)
                nc.vector.tensor_tensor(xl[u][:], x[u], f32(xh[u][:]), ALU.subtract).then_inc(x_low, 1)

            def subtract(j, u):
                b = 2 * j + u
                dve.wait_ge(part1, b + 1)
                atleast(dve, part3, b)
                nc.vector.tensor_tensor(rest[:], qk3[u], parts[u][:, :, 0, :], ALU.subtract).then_inc(remainder, 1)

            def third(j, u):
                dve.wait_ge(part2, 2 * j + u + 1)
                nc.vector.tensor_tensor(parts[u][:, :, 2, :], rest[:], parts[u][:, :, 1, :], ALU.subtract).then_inc(part3, 1)

            def values(j, u):
                b = 2 * j + u
                dve.wait_ge(v_ready, b + 1)
                nc.vector.tensor_copy(dyn1(t.vs, QT * b, QT), vps[u][:, :].rearrange("p (q d) -> p q d", q=QT)).then_inc(v_used, 1)

            norm = [(-2, lambda j, u: hT.normalise(dve, j, u))] if ln is not None else []
            skewed(dve, norm + [(1, subtract), (-1, low), (1, third)] + ([(1, values)] if wv else []))

        @block.tensor
        def _(pe):
            def products(j, u):
                b = 2 * j + u
                pe.wait_ge(x_low, b + 1)
                atleast(pe, remainder, b - 1)
                for ot in range(KT):
                    for w, wt in enumerate(weights):
                        last = mm3(nc.tensor, qk[u][:, ot * wcols + w * S:ot * wcols + (w + 1) * S],
                                   lambda x, kt: wt[x][:, kt, ot * P:(ot + 1) * P],
                                   lambda y, kt: (xh, xl)[y][u][:, kt, :], range(KT))
                last.then_inc(qk_ready, 1)
                if wv:
                    atleast(pe, v_used, b - 1)
                    for qt in range(QT):
                        last = mm3(nc.tensor, vps[u][:, qt * D:(qt + 1) * D],
                                   lambda x, kt: (xh, xl)[x][u][:, kt, qt * P:(qt + 1) * P],
                                   lambda y, kt: wv[y][:, kt, :], range(KT))
                    last.then_inc(v_ready, 1)

            turns = [(-1, lambda j, u: hT.turn(pe, j, u))] if ln is not None else []
            skewed(pe, turns + [(0, products)])


class ln_tiles:

    def __init__(self, nc, ctx, sem, t, ln):
        sb = lambda n, s, d: ctx.enter_context(nc.sbuf_tensor(n + str(sem.n), s, d))
        self.nc, self.t = nc, t
        self.gamma, self.beta = ln
        self.cent = [sb(f"cent{u}", [P, QT, D], F32) for u in range(2)]
        self.h = [sb(f"h{u}", [P, QT, D], F32) for u in range(2)]
        self.ps = [ctx.enter_context(nc.psum_tensor(f"hT{u}{sem.n}", [P, 512], F32)) for u in range(2)]
        self.centred, self.normed, self.copied = sem("centred"), sem("normed"), sem("copied_back")
        self.turned = sem("turned")

    def normalise(self, dve, j, u):
        b = 2 * j + u
        t = self.t
        for qt in range(QT):
            n = QT * b + qt
            atleast(dve, self.normed, QT * (b - 2) + qt + 1)
            r = dyn1(t.res, n, 1)[:, 0, :]
            mean = dyn1(t.mean, n, 1)
            self.nc.vector.scalar_tensor_tensor(self.cent[u][:, qt, :], r, mean, self.gamma, ALU.subtract,
                                                ALU.mult).then_inc(self.centred, 1)
            dve.wait_ge(self.centred, n + 1)
            atleast(dve, self.copied, b - 1)
            atleast(dve, self.turned, b - 1)
            self.nc.vector.scalar_tensor_tensor(self.h[u][:, qt, :], self.cent[u][:, qt, :], dyn1(t.rstd, n, 1),
                                                self.beta, ALU.mult, ALU.add).then_inc(self.normed, 1)

    def copy_back(self, pool, j, u):
        b = 2 * j + u
        pool.wait_ge(self.normed, QT * b + QT)
        pool.nop(nofuse=True)
        self.nc.gpsimd.tensor_copy(dyn1(self.t.res, QT * b, QT), self.h[u][:]).then_inc(self.copied, 1)

    def turn(self, pe, j, u):
        b = 2 * j + u
        pe.wait_ge(self.normed, QT * b + QT)
        for kt in range(KT):
            for qt in range(QT):
                last = self.nc.tensor.transpose(self.ps[u][:, kt * S + qt * P:kt * S + (qt + 1) * P],
                                                self.h[u][:, qt, kt * P:(kt + 1) * P], self.t.ident[:])
        last.then_inc(self.turned, 1)


def attention(nc, ctx, sem, t, causal, wo, load_stacks, n_loads, v_all, x_dram):
    nk = P if causal else SC
    KV = QT if causal else 1
    skeys = KV * nk
    order = [h for tile in range(KT) for odd in range(2) for h in range(P // DH * tile + odd, P // DH * (tile + 1), 2)]
    units = [(qt, order[i:i + G // kts], kts) for qt in range(QT) for kts in [qt + 1 if causal else 1]
             for i in range(0, H, G // kts)]
    UB = len(units)
    last_of = {qt: max(u for u in range(UB) if units[u][0] == qt) for qt in range(QT)}
    first_of = {qt: min(u for u in range(UB) if units[u][0] == qt) for qt in range(QT)}
    NSC, NTU, NPT = 4, 2, 4
    LREC, LTURN, LEVAC, LAV, LSPLIT, LPROJ, LRES, LKEEP = (2, 5, 6, 7, 8, 9, 10, 11) if causal else (1, 4, 4, 5, 6, 8, 9, 10)
    sb = lambda n, s, d: ctx.enter_context(nc.sbuf_tensor(n + str(sem.n), s, d))
    ps = lambda n, c: ctx.enter_context(nc.psum_tensor(n + str(sem.n), [P, c], F32))
    sq = [sb(f"sq{u}", [KS, H, S], BF16) for u in range(2)]
    sk = [sb(f"sk{u}", [KS, H, skeys], BF16) for u in range(2)]
    prob = [sb(f"prob{i}", [P, G * nk], F32) for i in range(UB)]
    negmax = [sb(f"negmax{i}", [P, G], F32) for i in range(UB)]
    sums = [sb(f"sums{i}", [P, G], F32) for i in range(UB)]
    recip = [sb(f"recip{i}", [P, G], F32) for i in range(UB)]
    probT = [sb(f"probT{i}", [P, G, P], F32) for i in range(NPT)]
    vpad = [sb(f"vpad{i}", [P, KV, H, 2 * DH], F32) for i in range(2)]
    oh = [sb(f"oh{i}", [P, KT, P], F32R) for i in range(QT)]
    ol = [sb(f"ol{i}", [P, KT, P], F32R) for i in range(QT)]
    stat = sb("stat", [P, 6], F32)
    agg = sb("agg", [P, 2], F32)
    rstat = sb("rstat", [P, QT, D], F32)
    score = [ps(f"score{i}", 512) for i in range(NSC)]
    turn = [ps(f"turn{i}", 512) for i in range(NTU)]
    oy = [ps(f"oy{i}", 512) for i in range(QT)]
    if causal:
        xt = [sb(f"xt{i}", [P, QT, D], F32) for i in range(2)]
        x_loaded = [sem("xt_loaded") for _ in range(2)]
    stacked = [sem("stacked") for _ in range(2)]
    zeroed, s_vpad = sem("vpad_zeroed"), sem("v_spread")
    s_score, s_max, s_exp, s_recip, s_norm = (sem(n) for n in ("score_ready", "max_ready", "exp_ready", "recip_ready", "norm_ready"))
    s_turn, s_evac, s_av, s_oh, s_ol = (sem(n) for n in ("probT_ready", "probT_copied", "av_ready", "o_high", "o_low"))
    s_y, s_res, s_stat, s_agg, s_mv, s_keep = (sem(n) for n in ("y_ready", "res_ready", "stat_ready", "agg_ready", "mv_ready", "res_kept"))

    def steps(eng, items):
        def step(b, u, k, after=False):
            for fn, lag in items:
                v = u - lag
                c = b + v // UB
                if isinstance(c, int) and (c < 0 or c >= B):
                    continue
                fn(c, v % UB, (k + v // UB) % 2)

        for k in range(2):
            for u in range(UB):
                step(k, u, k)
        with eng.Fori(1, B // 2) as j:
            for k in range(2):
                for u in range(UB):
                    step(2 * j + k, u, k)
        for i in range(max(lag for _, lag in items)):
            step(B + i // UB, i % UB, i // UB % 2)

    def pair_count(b, k, each):
        return each * (b // 2 + 1) if isinstance(b, int) else each // 2 * (b - k) + each

    with nc.Block() as block:
        @block.sync
        def _(sp):
            def body(j, k):
                b = 2 * j + k
                atleast(sp, s_score, UB * (b - 1))
                load_stacks(sp, b, sq[k], sk[k], stacked[k])
                if causal:
                    atleast(sp, s_res, QT * (b - 1))
                    sp.dma_start(xt[k][:], dyn(x_dram, b)).then_inc(x_loaded[k], 16)
            pairs(sp, body)

        @block.tensor
        def _(pe):
            mt = nc.tensor.matmul

            def scores(b, u, k):
                qt, heads, kts = units[u]
                w, out = kts * nk, score[u % NSC]
                if u == 0:
                    pe.wait_ge(stacked[k], pair_count(b, k, 16 * n_loads))
                atleast(pe, s_exp, UB * b + u - NSC + 1)
                if causal:
                    diag = out[:].rearrange("p (h k) -> p h k", h=len(heads))[:, :, w - P:w]
                    mt(diag, t.identb[:], t.maskb[:, 0:len(heads), :], start=True, stop=False, skip_group_check=True)
                for i, h in enumerate(heads):
                    last = mt(out[:, i * w:(i + 1) * w], sq[k][:, h, qt * P:(qt + 1) * P], sk[k][:, h, 0:w],
                              start=not causal, stop=True, skip_group_check=True)
                last.then_inc(s_score, 1)

            def transposes(b, u, k):
                qt, heads, kts = units[u]
                n = UB * b + u
                pe.wait_ge(s_norm, n + 1)
                atleast(pe, s_evac, n - NTU + 1)
                for i in range(len(heads) * kts):
                    last = nc.tensor.transpose(turn[u % NTU][0:nk, i * P:(i + 1) * P], prob[u][:, i * nk:(i + 1) * nk], t.ident[:])
                last.then_inc(s_turn, 1)

            def av(b, u, k):
                qt, heads, kts = units[u]
                if u == first_of[qt]:
                    atleast(pe, s_res, QT * (b - 1) + qt + 1)
                if u == 0:
                    pe.wait_ge(s_vpad, 2 * KV * (b + 1))
                pe.wait_ge(s_evac, UB * b + u + 1)
                for kt in range(kts):
                    for i, h in enumerate(heads):
                        tile, q = divmod(h // 2 * 2, P // DH)
                        rows = slice(DH * q, DH * (q + 2))
                        last = mt(oy[qt][rows, tile * P:(tile + 1) * P], vpad[k][0:nk, kt, h, :],
                                  probT[u % NPT][0:nk, i * kts + kt, :], start=h % 2 == 0 and kt == 0,
                                  stop=h % 2 == 1 and kt == kts - 1, skip_group_check=True)
                last.then_inc(s_av, 1)

            def project_out(b, u, k):
                qt = units[u][0]
                if u == last_of[qt]:
                    pe.wait_ge(s_ol, QT * b + qt + 1)
                    mm3(nc.tensor, oy[qt][:, D:2 * D], lambda x, kt: (oh, ol)[x][qt][:, kt, :],
                        lambda y, kt: wo[y][:, kt, :], range(KT)).then_inc(s_y, 1)

            steps(pe, [(scores, 0), (transposes, LTURN), (av, LAV), (project_out, LPROJ)])

        @block.scalar
        def _(act):
            def exps(b, u, k):
                qt, heads, kts = units[u]
                w = kts * nk
                act.wait_ge(s_max, UB * b + u + 1)
                atleast(act, s_turn, UB * (b - 1) + u + 1)
                atleast(act, s_recip, UB * (b - 1) + u + 1)
                for h in range(len(heads)):
                    last = nc.scalar.activation(prob[u][:, h * w:(h + 1) * w], score[u % NSC][:, h * w:(h + 1) * w],
                                                ACT.Exp, bias=negmax[u][:, h:h + 1], accum_out=sums[u][:, h:h + 1])
                last.then_inc(s_exp, 1)

            def high(b, u, k):
                qt = units[u][0]
                if u == last_of[qt]:
                    act.wait_ge(s_av, UB * b + u + 1)
                    atleast(act, s_y, QT * (b - 1) + qt + 1)
                    nc.scalar.activation(oh[qt][:], oy[qt][:, 0:D].rearrange("p (k q) -> p k q", k=KT),
                                         ACT.Copy).then_inc(s_oh, 1)

            def keep(b, u, k):
                qt = units[u][0]
                if u == last_of[qt]:
                    n = QT * b + qt
                    act.wait_ge(s_res, n + 1)
                    nc.scalar.activation(dyn1(t.res, n, 1)[:, 0, :], rstat[:, qt, :], ACT.Copy).then_inc(s_keep, 1)

            steps(act, [(high, LSPLIT), (exps, 0), (keep, LKEEP)])

        @block.gpsimd
        def _(pool):
            for v in vpad:
                nc.gpsimd.memset(v[:], 0.0).then_inc(zeroed, 1)
            pool.wait_ge(zeroed, 2)

            def spread(b, u, k):
                if u < 2 * KV:
                    kt, e = divmod(u, 2)
                    if u == 0:
                        atleast(pool, s_av, UB * (b - 1))
                        pool.nop(nofuse=True)
                    src = dyn1(v_all, KV * b + kt, 1)[:, 0, :].rearrange("p (m e d) -> p m e d", e=2, d=DH)[:, :, e, :]
                    dst = vpad[k][0:nk, kt, :, :].rearrange("p (m e) c -> p m e c", e=2)[:, :, e, e * DH:(e + 1) * DH]
                    nc.gpsimd.tensor_copy(dst, src).then_inc(s_vpad, 1)

            def normalise(b, u, k):
                qt, heads, kts = units[u]
                pool.wait_ge(s_recip, UB * b + u + 1)
                v = prob[u][:].rearrange("p (h k) -> p h k", h=len(heads))
                nc.gpsimd.tensor_tensor(v, v, recip[u][:, 0:len(heads)].unsqueeze(2).broadcast_to([P, len(heads), kts * nk]),
                                        ALU.mult).then_inc(s_norm, 1)

            steps(pool, [(normalise, 0), (spread, 0)])

        @block.vector
        def _(dve):
            def maxes(b, u, k):
                qt, heads, kts = units[u]
                dve.wait_ge(s_score, UB * b + u + 1)
                atleast(dve, s_exp, UB * (b - 1) + u + 1)
                nc.vector.tensor_reduce(negmax[u][:, 0:len(heads)],
                                        score[u % NSC][:, 0:G * nk].rearrange("p (h k) -> p h k", h=len(heads)),
                                        AX.X, ALU.max, negate=True).then_inc(s_max, 1)

            def recips(b, u, k):
                m = len(units[u][1])
                dve.wait_ge(s_exp, UB * b + u + 1)
                atleast(dve, s_norm, UB * (b - 1) + u + 1)
                nc.vector.reciprocal(recip[u][:, 0:m], sums[u][:, 0:m]).then_inc(s_recip, 1)

            def evac(b, u, k):
                n = UB * b + u
                dve.wait_ge(s_turn, n + 1)
                atleast(dve, s_av, n - NPT + 1)
                nc.vector.tensor_copy(probT[u % NPT][0:nk, :, :],
                                      turn[u % NTU][0:nk, :].rearrange("p (h q) -> p h q", h=G)).then_inc(s_evac, 1)

            def low(b, u, k):
                qt = units[u][0]
                if u == last_of[qt]:
                    dve.wait_ge(s_oh, QT * b + qt + 1)
                    nc.vector.tensor_tensor(ol[qt][:], oy[qt][:, 0:D].rearrange("p (k q) -> p k q", k=KT),
                                            f32(oh[qt][:]), ALU.subtract).then_inc(s_ol, 1)

            def residual(b, u, k):
                qt = units[u][0]
                if u == last_of[qt]:
                    n = QT * b + qt
                    dve.wait_ge(s_y, n + 1)
                    if causal:
                        dve.wait_ge(x_loaded[k], pair_count(b, k, 16))
                    atleast(dve, s_keep, QT * (b - 1) + qt + 1)
                    nc.vector.tensor_tensor(rstat[:, qt, :], oy[qt][:, D:2 * D],
                                            xt[k][:, qt, :] if causal else dyn1(t.res, n, 1)[:, 0, :], ALU.add).then_inc(s_res, 1)

            def statistic(b, u, k):
                qt = units[u][0]
                if u == last_of[qt]:
                    n = QT * b + qt
                    dve.wait_ge(s_res, n + 1)
                    atleast(dve, s_agg, n)
                    nc.vector.bn_stats(stat[:], rstat[:, qt, :]).then_inc(s_stat, 1)

            def aggregate(b, u, k):
                qt = units[u][0]
                if u == last_of[qt]:
                    n = QT * b + qt
                    dve.wait_ge(s_stat, n + 1)
                    atleast(dve, s_mv, n)
                    dve.nop(nofuse=True)
                    nc.vector.bn_aggr(agg[:], stat[:]).then_inc(s_agg, 1)

            def statistics_out(b, u, k):
                qt = units[u][0]
                if u == last_of[qt]:
                    n = QT * b + qt
                    dve.wait_ge(s_agg, n + 1)
                    nc.vector.tensor_copy(dyn1(t.mv, n, 1)[:, 0, :], agg[:]).then_inc(s_mv, 1)

            steps(dve, [(residual, LRES), (maxes, 0), (statistic, LRES), (evac, LEVAC), (aggregate, LRES), (recips, LREC),
                        (statistics_out, LRES), (low, LSPLIT)])


def statistics(nc, dve, t, n, r, stat, agg, s_res, s_stat, s_agg, s_mv):
    dve.wait_ge(s_res, n + 1)
    atleast(dve, s_agg, n)
    nc.vector.bn_stats(stat[:], r).then_inc(s_stat, 1)
    dve.wait_ge(s_stat, n + 1)
    atleast(dve, s_mv, n)
    dve.nop(nofuse=True)
    nc.vector.bn_aggr(agg[:], stat[:]).then_inc(s_agg, 1)
    dve.wait_ge(s_agg, n + 1)
    nc.vector.tensor_copy(dyn1(t.mv, n, 1)[:, 0, :], agg[:]).then_inc(s_mv, 1)


def finish_stats(nc, sem, t):
    mean_done, std_done, eps_done, done = sem("mean"), sem("std"), sem("std_eps"), sem("rstd")
    with nc.Block() as block:
        @block.scalar
        def _(act):
            nc.scalar.activation(t.std[:], t.mv[:, :, 1], ACT.Sqrt, scale=D / (D - 1.0)).then_inc(std_done, 1)

        @block.vector
        def _(dve):
            nc.vector.tensor_copy(t.mean[:], t.mv[:, :, 0]).then_inc(mean_done, 1)
            dve.wait_ge(std_done, 1)
            nc.vector.tensor_scalar(t.rstd[:], t.std[:], EPS, None, ALU.add).then_inc(eps_done, 1)
            dve.wait_ge(eps_done, 1)
            nc.vector.reciprocal(t.rstd[:], t.rstd[:]).then_inc(done, 1)


def feed_forward(nc, ctx, sem, t, w1, w2, b1, b2, ln):
    sb = lambda n, s, d: ctx.enter_context(nc.sbuf_tensor(n + str(sem.n), s, d))
    ps = lambda n: ctx.enter_context(nc.psum_tensor(n + str(sem.n), [P, 512], F32))
    hT = ln_tiles(nc, ctx, sem, t, ln)
    xh = [sb(f"fxh{u}", [P, KT, S], F32R) for u in range(2)]
    xl = [sb(f"fxl{u}", [P, KT, S], F32R) for u in range(2)]
    hid = [sb(f"hid{u}", [P, 2, S], F32) for u in range(2)]
    hh = [sb(f"hh{u}", [P, FT, S], F32R) for u in range(2)]
    hl = [sb(f"hl{u}", [P, FT, S], F32R) for u in range(2)]
    part = sb("ffpart", [P, D], F32)
    stat = sb("ffstat", [P, 6], F32)
    agg = sb("ffagg", [P, 2], F32)
    rstat = sb("ffrstat", [P, QT, D], F32)
    s_mv, s_keep = sem("ff_mv"), sem("ff_kept")
    up = [ps(f"up{i}") for i in range(2)]
    down = [ps(f"down{i}") for i in range(QT)]
    s_xh, s_xl, s_up, s_hid, s_hh, s_hl = sem("ff_xh"), sem("ff_xl"), sem("up_ready"), sem("hid_ready"), sem("hid_high"), sem("hid_low")
    s_down, s_part, s_res, s_stat, s_agg = sem("down_ready"), sem("ff_part"), sem("ff_res"), sem("ff_stat"), sem("ff_agg")

    with nc.Block() as block:
        @block.tensor
        def _(pe):
            def down_step(j, u):
                b = 2 * j + u
                for qt in range(QT):
                    atleast(pe, s_res, QT * (b - 1) + qt + 1)
                    pe.wait_ge(s_hl, FT // 2 * (b + 1))
                    mm3(nc.tensor, down[qt][:, 0:D], lambda x, m: (hh, hl)[x][u][:, m, qt * P:(qt + 1) * P],
                        lambda y, m: w2[y][:, m, :], range(FT)).then_inc(s_down, 1)

            def body(j, u, more=True):
                b = 2 * j + u
                pe.wait_ge(s_xl, b + 1)
                for m2 in range(FT // 2):
                    n = FT // 2 * b + m2
                    atleast(pe, s_hid, n - 1)
                    for m in (2 * m2, 2 * m2 + 1):
                        last = mm3(nc.tensor, up[m2 % 2][:, m % 2 * S:(m % 2 + 1) * S],
                                   lambda x, kt: w1[x][:, kt, m * P:(m + 1) * P],
                                   lambda y, kt: (xh, xl)[y][u][:, kt, :], range(KT))
                    last.then_inc(s_up, 1)
                    if m2 == 1 and more:
                        hT.turn(pe, *((j + 1, 0) if u else (j, 1)))
                if not (isinstance(j, int) and j == 0 and u == 0):
                    down_step(*((j, 0) if u else (j - 1, 1)))

            hT.turn(pe, 0, 0)
            for u in range(2):
                body(0, u)
            with pe.Fori(1, B // 2 - 1) as j:
                for u in range(2):
                    body(j, u)
            body(B // 2 - 1, 0)
            body(B // 2 - 1, 1, False)
            down_step(B // 2 - 1, 1)

        @block.scalar
        def _(act):
            def body(j, u):
                b = 2 * j + u
                act.wait_ge(hT.turned, b + 1)
                atleast(act, s_up, FT // 2 * (b - 1))
                nc.scalar.activation(xh[u][:], hT.ps[u][:, :].rearrange("p (k s) -> p k s", k=KT), ACT.Copy).then_inc(s_xh, 1)
                for m2 in range(FT // 2):
                    n = FT // 2 * b + m2
                    act.wait_ge(s_up, n + 1)
                    atleast(act, s_hl, n - 1)
                    for m in range(2):
                        last = nc.scalar.activation(hid[m2 % 2][:, m, :], up[m2 % 2][:, m * S:(m + 1) * S], ACT.Relu,
                                                    bias=b1[:, 2 * m2 + m:2 * m2 + m + 1])
                    last.then_inc(s_hid, 1)
                    act.wait_ge(s_hid, n + 1)
                    if m2 == 0:
                        atleast(act, s_down, QT * (b - 1))
                    nc.scalar.activation(hh[u][:, 2 * m2:2 * m2 + 2, :], hid[m2 % 2][:], ACT.Copy).then_inc(s_hh, 1)
                    if m2 == 2 and not (isinstance(j, int) and j == 0 and u == 0):
                        keep(*((j, 0) if u else (j - 1, 1)), late=1)

            def keep(j, u, late=0):
                for qt in range(QT):
                    n = QT * (2 * j + u) + qt
                    if late:
                        n = n - QT
                        if isinstance(n, int) and n < 0:
                            continue
                    act.wait_ge(s_res, n + 1)
                    nc.scalar.activation(dyn1(t.res, n, 1)[:, 0, :], rstat[:, qt, :], ACT.Copy).then_inc(s_keep, 1)
            pairs(act, body)
            keep(B // 2 - 1, 0)
            keep(B // 2 - 1, 1)

        @block.gpsimd
        def _(pool):
            def body(j, u):
                b = 2 * j + u
                hT.copy_back(pool, j, u)
            pairs(pool, body)

        @block.vector
        def _(dve):
            def finish(j, u):
                b = 2 * j + u
                for qt in range(QT):
                    n = QT * b + qt
                    r = dyn1(t.res, n, 1)[:, 0, :]
                    dve.wait_ge(s_down, n + 1)
                    dve.wait_ge(hT.copied, b + 1)
                    atleast(dve, s_res, n)
                    nc.vector.tensor_tensor(part[:], down[qt][:, 0:D], b2[:], ALU.add).then_inc(s_part, 1)
                    dve.wait_ge(s_part, n + 1)
                    atleast(dve, s_keep, QT * (b - 1) + qt + 1)
                    nc.vector.tensor_tensor(rstat[:, qt, :], part[:], r, ALU.add).then_inc(s_res, 1)
                    statistics(nc, dve, t, n, rstat[:, qt, :], stat, agg, s_res, s_stat, s_agg, s_mv)

            def low(j, u):
                b = 2 * j + u
                dve.wait_ge(s_xh, b + 1)
                nc.vector.tensor_tensor(xl[u][:], hT.ps[u][:, :].rearrange("p (k s) -> p k s", k=KT),
                                        f32(xh[u][:]), ALU.subtract).then_inc(s_xl, 1)

            def hidden(j, u, m2):
                n = FT // 2 * (2 * j + u) + m2
                dve.wait_ge(s_hh, n + 1)
                nc.vector.tensor_tensor(hl[u][:, 2 * m2:2 * m2 + 2, :], hid[m2 % 2][:], f32(hh[u][:, 2 * m2:2 * m2 + 2, :]),
                                        ALU.subtract).then_inc(s_hl, 1)

            def body(j, u, more=True):
                if more:
                    hT.normalise(dve, *((j + 1, 0) if u else (j, 1)))
                for m2 in range(FT // 2):
                    hidden(j, u, m2)
                if more:
                    low(j, 1) if u == 0 else low(j + 1, 0)
                if not (isinstance(j, int) and j == 0 and u == 0):
                    finish(*((j, 0) if u else (j - 1, 1)))

            hT.normalise(dve, 0, 0)
            low(0, 0)
            for u in range(2):
                body(0, u)
            with dve.Fori(1, B // 2 - 1) as j:
                for u in range(2):
                    body(j, u)
            body(B // 2 - 1, 0)
            body(B // 2 - 1, 1, False)
            finish(B // 2 - 1, 1)


def replicate_column(nc, ctx, sem, col, rep):
    zero = ctx.enter_context(nc.sbuf_tensor("zeros", [P, P], F32))
    full = ctx.enter_context(nc.sbuf_tensor("rep_full", [P, KT, P], F32))
    zeroed, filled, rounded, split = (sem(n) for n in ("zeroed", "filled", "rounded", "rep_split"))
    with nc.Block() as block:
        @block.vector
        def _(dve):
            nc.vector.memset(zero[:], 0.0).then_inc(zeroed, 1)
            dve.wait_ge(zeroed, 1)
            for kt in range(KT):
                nc.vector.tensor_scalar(full[:, kt, :], zero[:], col[:, kt:kt + 1], None, ALU.add).then_inc(filled, 1)
            dve.wait_ge(filled, KT)
            nc.vector.tensor_copy(rep[0][:], full[:]).then_inc(rounded, 1)
            dve.wait_ge(rounded, 1)
            nc.vector.tensor_tensor(rep[1][:], full[:], f32(rep[0][:]), ALU.subtract).then_inc(split, 1)


class Job:

    def __init__(self, rows, cols, stat, mov, full=None, halves=None, scale=1.0, col=None, row=None, after=0):
        self.rows, self.cols, self.stat, self.mov, self.full, self.halves = rows, cols, stat, mov, full, halves
        self.scale, self.col, self.row, self.after = scale, col, row, after


def product_jobs(nc, ctx, sem, jobs):
    NB = 4
    ps = [ctx.enter_context(nc.psum_tensor(f"job{i}_{sem.n}", [P, 512], F32)) for i in range(NB)]
    stage = ctx.enter_context(nc.sbuf_tensor(f"jobf_{sem.n}", [P, 512], F32))
    made, staged, high, done = (sem(n) for n in ("job_made", "job_staged", "job_high", "job_done"))

    def before(n, kind):
        return sum(map(kind, jobs[:n]))

    halved = lambda job: job.halves is not None
    via_stage = lambda job: halved(job) and job.row is not None

    def source(n, o):
        job = jobs[n]
        v = (stage if via_stage(job) else ps[n % NB])[0:job.rows, 0:job.cols]
        return v if len(o.shape) == 2 else v.rearrange("p (b k) -> p b k", k=SC)

    with nc.Block() as block:
        @block.tensor
        def _(pe):
            for n, job in enumerate(jobs):
                if max(n - NB + 1, job.after) > 0:
                    pe.wait_ge(done, max(n - NB + 1, job.after))
                mm3(nc.tensor, ps[n % NB][0:job.rows, 0:job.cols], job.stat, job.mov, range(KT)).then_inc(made, 1)

        @block.vector
        def _(dve):
            for n, job in enumerate(jobs):
                src = ps[n % NB][0:job.rows, 0:job.cols]
                dve.wait_ge(made, n + 1)
                if not halved(job):
                    if job.row is not None:
                        nc.vector.tensor_tensor(job.full, src, job.row, ALU.add).then_inc(done, 1)
                    else:
                        nc.vector.tensor_scalar(job.full, src, job.scale, None, ALU.mult).then_inc(done, 1)
                    continue
                if via_stage(job):
                    if n:
                        dve.wait_ge(done, n)
                    nc.vector.tensor_tensor(stage[0:job.rows, 0:job.cols], src, job.row, ALU.add).then_inc(staged, 1)
                hi, lo = job.halves
                dve.wait_ge(high, before(n + 1, halved))
                if via_stage(job):
                    nc.vector.tensor_tensor(lo, source(n, lo), f32(hi), ALU.subtract).then_inc(done, 1)
                elif job.col is not None:
                    nc.vector.scalar_tensor_tensor(lo, source(n, lo), job.col, f32(hi), ALU.add, ALU.subtract).then_inc(done, 1)
                else:
                    nc.vector.scalar_tensor_tensor(lo, source(n, lo), job.scale, f32(hi), ALU.mult, ALU.subtract).then_inc(done, 1)

        @block.scalar
        def _(act):
            for n, job in enumerate(jobs):
                if halved(job):
                    hi = job.halves[0]
                    if via_stage(job):
                        act.wait_ge(staged, before(n + 1, via_stage))
                    else:
                        act.wait_ge(made, n + 1)
                    if job.col is not None:
                        nc.scalar.activation(hi, source(n, hi), ACT.Identity, bias=job.col).then_inc(high, 1)
                    else:
                        nc.scalar.activation(hi, source(n, hi), ACT.Copy, scale=1.0 if via_stage(job) else job.scale).then_inc(high, 1)


def gated_prep_scores(nc, ctx, sem, t, g):
    c, jobs = (t.ch, t.cl), []
    for ot in range(KT):
        o = slice(ot * P, (ot + 1) * P)
        for c0, cn in CCH:
            jobs.append(Job(P, cn, lambda x, kt, o=o: g.wk[x][:, kt, o], lambda y, kt, c0=c0, cn=cn: c[y][:, kt, c0:c0 + cn],
                            halves=[k[:, ot, c0:c0 + cn] for k in g.kp], col=g.bk[:, ot:ot + 1]))
    n_kp = len(jobs)
    kp = lambda c0, cn: lambda y, kt: g.kp[y][:, kt, c0:c0 + cn]
    rep = lambda x, kt: g.rep[x][:, kt, :]
    for ot in range(KT):
        o = slice(ot * P, (ot + 1) * P)
        for c0, cn in CCH:
            jobs.append(Job(P, cn, lambda x, kt, o=o: g.wqT[x][:, kt, o], kp(c0, cn), scale=SCALE, after=n_kp,
                            halves=[v[:, ot, c0 // SC:(c0 + cn) // SC, 0:SC] for v in g.a]))
        jobs.append(Job(P, D, lambda x, kt, o=o: g.wqT[x][:, kt, o], lambda y, kt: g.wg1[y][:, kt, :],
                        halves=[v[:, ot, :] for v in g.wqg]))
    for c0, cn in CCH:
        jobs.append(Job(P, cn, rep, kp(c0, cn), scale=SCALE, full=g.cb[:, c0:c0 + cn]))
    jobs.append(Job(P, D, rep, lambda y, kt: g.wg1[y][:, kt, :], full=g.gb[:], row=g.bg[:]))
    product_jobs(nc, ctx, sem, jobs)


def gated_prep_values(nc, ctx, sem, t, g):
    c, jobs = (t.ch, t.cl), []
    for ot in range(KT):
        o = slice(ot * P, (ot + 1) * P)
        for c0, cn in CCH:
            jobs.append(Job(P, cn, lambda x, kt, o=o: g.wv[x][:, kt, o], lambda y, kt, c0=c0, cn=cn: c[y][:, kt, c0:c0 + cn],
                            halves=[k[:, ot, c0:c0 + cn] for k in g.vpT], col=g.bv[:, ot:ot + 1]))
    n_vp = len(jobs)
    for b in range(B):
        k = slice(b * SC, (b + 1) * SC)
        jobs.append(Job(SC, D, lambda x, kt, k=k: c[x][:, kt, k], lambda y, kt: g.wv[y][:, kt, :], row=g.bvr[0:SC, :],
                        halves=[v[:, b, 0:D] for v in g.vv]))
        jobs.append(Job(SC, D, lambda x, kt, k=k: g.vpT[x][:, kt, k], lambda y, kt: g.wg2[y][:, kt, :], after=n_vp,
                        halves=[v[:, b, D:2 * D] for v in g.vv]))
    product_jobs(nc, ctx, sem, jobs)


def gated_attention(nc, ctx, sem, t, g, ln, mask, out):
    sb = lambda n, s, d: ctx.enter_context(nc.sbuf_tensor(n + str(sem.n), s, d))
    ps = lambda n: ctx.enter_context(nc.psum_tensor(n + str(sem.n), [P, 512], F32))
    hT = ln_tiles(nc, ctx, sem, t, ln)
    xh = [sb(f"gxh{u}", [P, KT, S], F32R) for u in range(2)]
    xl = [sb(f"gxl{u}", [P, KT, S], F32R) for u in range(2)]
    s_sb, p_sb = sb("gs", [P, QT, SC], F32), [sb(f"gp{u}", [P, QT, SC], F32) for u in range(2)]
    nmax, sums, rec = sb("gnm", [P, QT], F32), sb("gsum", [P, QT], F32), sb("grec", [P, QT], F32)
    pth, ptl = sb("gpth", [SC, QT, P], F32R), sb("gptl", [SC, QT, P], F32R)
    gq_sb = [sb(f"ggq{u}", [P, QT, D], F32) for u in range(2)]
    gate, tanh, gated = (sb(n, [P, QT, D], F32) for n in ("gate", "gtanh", "gated"))
    half_mask = sb("half_mask", [P, NT], F32)
    fin = [sb(f"fin{u}", [P, QT, D], F32) for u in range(2)]
    sc, gq, pt = ps("gsc"), ps("ggqp"), ps("gpt")
    xo = ctx.enter_context(nc.psum_tensor("gxo", [P, QT, 2 * D], F32))
    names = ("g_xh", "g_xl", "g_sc", "g_s", "g_max", "g_gq", "g_gqb", "g_exp", "g_rec", "g_p", "g_pt", "g_pth", "g_ptl",
             "g_xo", "g_gate", "g_tanh", "g_gated", "g_fin", "half_mask_made")
    (s_xh, s_xl, s_sc, s_s, s_max, s_gq, s_gqb, s_exp, s_rec, s_p, s_pt, s_pth, s_ptl, s_xo, s_gate, s_tanh,
     s_gated, s_fin, s_half) = (sem(n) for n in names)
    stored = [sem("out_stored") for _ in range(2)]

    with nc.Block() as block:
        @block.tensor
        def _(pe):
            def turn_p(j, u):
                b = 2 * j + u
                pe.wait_ge(s_p, QT * (b + 1))
                atleast(pe, s_ptl, b)
                for q in range(QT):
                    last = nc.tensor.transpose(pt[0:SC, q * P:(q + 1) * P], p_sb[u][:, q, :], t.ident[:])
                last.then_inc(s_pt, 1)

            def scores(j, u):
                b = 2 * j + u
                pe.wait_ge(s_xl, b + 1)
                atleast(pe, s_s, b)
                for q in range(QT):
                    last = mm3(nc.tensor, sc[:, q * SCE:(q + 1) * SCE], lambda x, kt: (xh, xl)[x][u][:, kt, q * P:(q + 1) * P],
                               lambda y, kt: dyn1(g.a[y][:, kt, :, :], b, 1)[:, 0, :], range(KT))
                last.then_inc(s_sc, 1)

            def gates(j, u):
                b = 2 * j + u
                atleast(pe, s_gqb, b)
                for q in range(QT):
                    last = mm3(nc.tensor, gq[:, q * D:(q + 1) * D], lambda x, kt: (xh, xl)[x][u][:, kt, q * P:(q + 1) * P],
                               lambda y, kt: g.wqg[y][:, kt, :], range(KT))
                last.then_inc(s_gq, 1)

            def mix(j, u):
                b = 2 * j + u
                pe.wait_ge(s_ptl, b + 1)
                atleast(pe, s_gated, b)
                for q in range(QT):
                    last = mm3(nc.tensor, xo[:, q, :], lambda x, kt: (pth, ptl)[x][:, q, :],
                               lambda y, kt: dyn1(g.vv[y], b, 1)[:, 0, :], range(1))
                last.then_inc(s_xo, 1)

            skewed(pe, [(-1, lambda j, u: hT.turn(pe, j, u)), (1, turn_p), (0, scores), (0, gates), (1, mix)])

        @block.scalar
        def _(act):
            def high(j, u):
                act.wait_ge(hT.turned, 2 * j + u + 1)
                atleast(act, s_gq, 2 * j + u - 1)
                nc.scalar.activation(xh[u][:], hT.ps[u][:, :].rearrange("p (k s) -> p k s", k=KT), ACT.Copy).then_inc(s_xh, 1)

            def p_high(j, u):
                b = 2 * j + u
                act.wait_ge(s_pt, b + 1)
                atleast(act, s_xo, b)
                nc.scalar.activation(pth[:], pt[0:SC, 0:S].rearrange("p (q s) -> p q s", q=QT), ACT.Copy).then_inc(s_pth, 1)

            def exps(j, u):
                b = 2 * j + u
                act.wait_ge(s_max, b + 1)
                atleast(act, s_pt, b - 1)
                atleast(act, s_rec, b)
                for q in range(QT):
                    last = nc.scalar.activation(p_sb[u][:, q, :], s_sb[:, q, :], ACT.Exp, bias=nmax[:, q:q + 1],
                                                accum_out=sums[:, q:q + 1])
                last.then_inc(s_exp, 1)

            def gate_tanh(j, u):
                b = 2 * j + u
                act.wait_ge(s_gate, b + 1)
                atleast(act, s_gated, b)
                nc.scalar.activation(tanh[:], gate[:], ACT.Tanh, scale=0.5).then_inc(s_tanh, 1)

            skewed(act, [(2, gate_tanh), (-1, high), (1, p_high), (0, exps)])

        @block.vector
        def _(dve):
            def low(j, u):
                dve.wait_ge(s_xh, 2 * j + u + 1)
                nc.vector.tensor_tensor(xl[u][:], hT.ps[u][:, :].rearrange("p (k s) -> p k s", k=KT), f32(xh[u][:]),
                                        ALU.subtract).then_inc(s_xl, 1)

            def p_low(j, u):
                dve.wait_ge(s_pth, 2 * j + u + 1)
                nc.vector.tensor_tensor(ptl[:], pt[0:SC, 0:S].rearrange("p (q s) -> p q s", q=QT), f32(pth[:]),
                                        ALU.subtract).then_inc(s_ptl, 1)

            def shifted(j, u):
                b = 2 * j + u
                dve.wait_ge(s_sc, b + 1)
                atleast(dve, s_exp, b)
                nc.vector.tensor_tensor(s_sb[:], sc[:, 0:QT * SCE].rearrange("p (q k) -> p q k", q=QT)[:, :, 0:SC],
                                        dyn1(g.cb[:].rearrange("p (b k) -> p b k", k=SC), b, 1).broadcast_to([P, QT, SC]),
                                        ALU.add).then_inc(s_s, 1)
                dve.wait_ge(s_s, b + 1)
                nc.vector.tensor_reduce(nmax[:], s_sb[:], AX.X, ALU.max, negate=True).then_inc(s_max, 1)

            def gate_q(j, u):
                b = 2 * j + u
                dve.wait_ge(s_gq, b + 1)
                atleast(dve, s_gate, b - 1)
                nc.vector.tensor_tensor(gq_sb[u][:], gq[:].rearrange("p (q d) -> p q d", q=QT),
                                        g.gb[:].unsqueeze(1).broadcast_to([P, QT, D]), ALU.add).then_inc(s_gqb, 1)

            def scale_p(j, u):
                b = 2 * j + u
                dve.wait_ge(s_exp, b + 1)
                nc.vector.reciprocal(rec[:], sums[:]).then_inc(s_rec, 1)
                dve.wait_ge(s_rec, b + 1)
                for q in range(QT):
                    nc.vector.tensor_scalar(p_sb[u][:, q, :], p_sb[u][:, q, :], rec[:, q:q + 1], None, ALU.mult).then_inc(s_p, 1)

            def gate_sum(j, u):
                b = 2 * j + u
                dve.wait_ge(s_xo, b + 1)
                atleast(dve, s_tanh, b)
                nc.vector.tensor_tensor(gate[:], xo[:, :, D:2 * D], gq_sb[u][:], ALU.add).then_inc(s_gate, 1)

            def gate_x(j, u):
                b = 2 * j + u
                dve.wait_ge(s_tanh, b + 1)
                atleast(dve, s_fin, QT * b)
                nc.vector.scalar_tensor_tensor(gated[:], tanh[:], 1.0, xo[:, :, 0:D], ALU.add,
                                               ALU.mult).then_inc(s_gated, 1)

            def finish(j, u):
                b = 2 * j + u
                dve.wait_ge(s_gated, b + 1)
                dve.wait_ge(hT.copied, b + 1)
                atleast(dve, stored[u], 16 * j)
                for q in range(QT):
                    n = QT * b + q
                    nc.vector.scalar_tensor_tensor(fin[u][:, q, :], gated[:, q, :], dyn1(half_mask[:], n, 1),
                                                   dyn1(t.res, n, 1)[:, 0, :], ALU.mult, ALU.add).then_inc(s_fin, 1)

            nc.vector.tensor_scalar(half_mask[:], mask[:], 0.5, None, ALU.mult).then_inc(s_half, 1)
            dve.wait_ge(s_half, 1)
            skewed(dve, [(2, gate_sum), (-1, low), (1, p_low), (2, gate_x), (0, shifted), (2, finish),
                         (-2, lambda j, u: hT.normalise(dve, j, u)), (0, scale_p), (0, gate_q)])

        @block.gpsimd
        def _(pool):
            skewed(pool, [(0, lambda j, u: hT.copy_back(pool, j, u))])

        @block.sync
        def _(sp):
            def body(j, u):
                b = 2 * j + u
                sp.wait_ge(s_fin, QT * (b + 1))
                sp.dma_start(dyn(out, b), fin[u][:]).then_inc(stored[u], 16)
            pairs(sp, body)
            for u in range(2):
                sp.wait_ge(stored[u], 16 * (B // 2))


class Tensors:
    pass


def program(nc, a, out):
    with ExitStack() as whole:
        sem = Sems(nc)
        run = sem.stage

        def sb(name, shape, dt, ctx=whole):
            return ctx.enter_context(nc.sbuf_tensor(name, shape, dt))

        t = Tensors()
        t.ident, t.identb = sb("ident", [P, P], F32), sb("identb", [P, P], BF16)
        t.maskb = sb("maskb", [P, G, P], BF16)
        t.res = sb("res", [P, NT, D], F32)
        t.mv, t.mean, t.std, t.rstd = sb("mv", [P, NT, 2], F32), sb("mean", [P, NT], F32), sb("std", [P, NT], F32), sb("rstd", [P, NT], F32)
        t.ch, t.cl = sb("ctx_high", [P, KT, CT], F32R), sb("ctx_low", [P, KT, CT], F32R)
        rows = {n: sb(n, [P, D], F32) for n in ("ln1_g", "ln1_b", "ln2_g", "ln2_b", "ln3_g", "ln3_b", "ff_b2", "bg", "bvr")}
        cols = {n: sb(n + "_col", [P, k], F32) for n, k in (("ff_b1", FT), ("bq", KT), ("bk", KT), ("bv", KT))}
        mask = sb("mask", [P, NT], F32)
        qk_dram = nc.dram_tensor("qk_parts", (B, KT, P, 3 * 2 * S), BF16).ap()
        q_dram = nc.dram_tensor("q_parts", (B, KT, P, 3 * S), BF16).ap()
        kc_dram = nc.dram_tensor("kc_parts", (KT, P, 3 * CT), BF16).ap()
        run(setup_constants, sem, t)

        small = whole.enter_context(nc.semaphore("small_loaded"))
        with nc.Block() as block:
            @block.sync
            def _(sp):
                n = 0
                src = dict(bg="L1_xattn_bg", bvr="L1_xattn_bv")
                for k, v in rows.items():
                    sp.dma_start(v[:], a[src.get(k, "L0_xattn_" + k)].partition_broadcast(P)).then_inc(small, 16)
                    n += 1
                for k, v in cols.items():
                    w = a[k + "_col"]
                    sp.dma_start(v[:], w).then_inc(small, 16)
                    n += 1
                sp.dma_start(mask[:], a["maskT"]).then_inc(small, 16)
                sp.wait_ge(small, 16 * (n + 1))

        def weights(ctx, names, kts, colsn):
            jobs, out_ = [], []
            for (name, ap, scale), kt, c in zip(names, kts, colsn):
                w = [sb(f"{name}{i}", [P, kt, c], F32R, ctx) for i in range(2)]
                jobs.append((ap, w[0][:], w[1][:], scale))
                out_.append(w)
            with ExitStack() as st:
                run(split_weights, st, sem, jobs)
            return out_

        def stacks(parts, kparts):
            def load(sp, b, sq, sk, s):
                for term, (pq, pk) in enumerate(TERMS):
                    rows_ = slice(term * DH, (term + 1) * DH)
                    v = dyn(parts, b).rearrange("k (m d) (t w s) -> t w d (k m) s", d=DH, t=3, s=S)
                    sp.dma_start(sq[rows_, :, :], v[pq, 0]).then_inc(s, 16)
                    if kparts is None:
                        sp.dma_start(sk[rows_, :, :], v[pk, 1]).then_inc(s, 16)
                    else:
                        kv = kparts.rearrange("k (m d) (t b s) -> b t d (k m) s", d=DH, t=3, s=SC)
                        sp.dma_start(sk[rows_, :, :], dyn(kv, b)[pk]).then_inc(s, 16)
            return load

        A = lambda n: a["L0_xattn_" + n]
        context = ExitStack()
        t.vc = sb("vc", [SC, B, D], F32, context)
        with ExitStack() as ctx:
            wk, wv = weights(ctx, [("cwk", A("ca_wk"), 1.0), ("cwv", A("ca_wv"), 1.0)], [KT] * 2, [D] * 2)
            with ExitStack() as st:
                run(split_context, st, sem, a["ctxT"], t.ch, t.cl)
            run(context_kv, ctx, sem, t, wk, wv, kc_dram)

        with ExitStack() as sa:
            t.vs = sb("vs", [P, NT, D], F32, sa)
            wo, = weights(sa, [("swo", A("sa_wo"), 1.0)], [KT], [D])
            with ExitStack() as ctx:
                wq, wk, wv = weights(ctx, [("swq", A("sa_wq"), SCALE), ("swk", A("sa_wk"), 1.0), ("swv", A("sa_wv"), 1.0)],
                                     [KT] * 3, [D] * 3)
                run(project, ctx, sem, t, a["xT"].rearrange("b (k p) s -> b p k s", p=P), [wq, wk],
                        qk_dram.rearrange("b k p c -> b p k c"), wv=wv)
            with ExitStack() as ctx:
                run(attention, ctx, sem, t, True, wo, stacks(qk_dram, None), 2 * NTERM, t.vs,
                          a["x"].rearrange("b (q p) d -> b p q d", p=P))
        run(finish_stats, sem, t)

        with ExitStack() as ca:
            wo, = weights(ca, [("cwo", A("ca_wo"), 1.0)], [KT], [D])
            with ExitStack() as ctx:
                wq, = weights(ctx, [("cwq", A("ca_wq"), SCALE)], [KT], [D])
                run(project, ctx, sem, t, None, [wq], q_dram.rearrange("b k p c -> b p k c"),
                        ln=(rows["ln1_g"][:], rows["ln1_b"][:]))
            with ExitStack() as ctx:
                run(attention, ctx, sem, t, False, wo, stacks(q_dram, kc_dram), 2 * NTERM, t.vc, None)
        context.close()
        run(finish_stats, sem, t)

        with ExitStack() as ctx:
            w1, w2 = weights(ctx, [("fw1", A("ff_w1"), 1.0), ("fw2", A("ff_w2"), 1.0)], [KT, FT], [F, D])
            run(feed_forward, ctx, sem, t, w1, w2, cols["ff_b1"], rows["ff_b2"], (rows["ln2_g"][:], rows["ln2_b"][:]))
        run(finish_stats, sem, t)

        with ExitStack() as ctx:
            g = Tensors()
            g.a = [sb(f"ga{i}", [P, KT, B, SCE], F32R, ctx) for i in range(2)]
            g.wqg = [sb(f"gwqg{i}", [P, KT, D], F32R, ctx) for i in range(2)]
            g.cb, g.gb = sb("gcb", [P, CT], F32, ctx), sb("ggb", [P, D], F32, ctx)
            g.bq, g.bk, g.bv, g.bg, g.bvr = cols["bq"], cols["bk"], cols["bv"], rows["bg"], rows["bvr"]
            spare = ctx.enter_context(nc.semaphore("spare_column"))
            with nc.Block() as block:
                @block.vector
                def _(dve):
                    for v in g.a:
                        nc.vector.memset(f32(v[:, :, :, SC:SCE]), 0.0).then_inc(spare, 1)
            with ExitStack() as st:
                g.kp = [sb(f"gkp{i}", [P, KT, CT], F32R, st) for i in range(2)]
                g.rep = [sb(f"bq_rep{i}", [P, KT, P], F32R, st) for i in range(2)]
                g.wqT, g.wk, g.wg1 = weights(st, [("gwqT", a["WqT"], 1.0), ("gwk", a["L1_xattn_Wk"], 1.0),
                                                  ("gwg1", a["L1_xattn_Wg"][0:D, :], 1.0)], [KT] * 3, [D] * 3)
                run(replicate_column, st, sem, g.bq, g.rep)
                run(gated_prep_scores, st, sem, t, g)
            g.vv = [sb(f"gvv{i}", [SC, B, 2 * D], F32R, ctx) for i in range(2)]
            with ExitStack() as st:
                g.vpT = [sb(f"gvpT{i}", [P, KT, CT], F32R, st) for i in range(2)]
                g.wv, g.wg2 = weights(st, [("gwv", a["L1_xattn_Wv"], 1.0), ("gwg2", a["L1_xattn_Wg"][D:2 * D, :], 1.0)],
                                      [KT] * 2, [D] * 2)
                run(gated_prep_values, st, sem, t, g)
            run(gated_attention, ctx, sem, t, g, (rows["ln3_g"][:], rows["ln3_b"][:]), mask,
                            out.rearrange("b (q p) d -> b p q d", p=P))


def kernel(**inputs):
    import numpy as np
    import concourse.bacc as bacc
    from concourse.bass_utils import run_bass_kernel_spmd

    nc = bacc.Bacc("TRN2", target_bir_lowering=False, num_devices=1)
    laid = {n: np.ascontiguousarray(v) for n, v in inputs.items()}
    laid["xT"] = np.ascontiguousarray(laid["x"].transpose(0, 2, 1))
    laid["ctxT"] = np.ascontiguousarray(laid.pop("ctx_1024").reshape(CT, D).T)
    laid["WqT"] = np.ascontiguousarray(laid.pop("L1_xattn_Wq").T)
    for n in ("sa_wq", "sa_wk", "sa_wv", "sa_wo", "ca_wq", "ca_wk", "ca_wv", "ca_wo", "ff_w1", "ff_w2"):
        laid["L0_xattn_" + n] = np.ascontiguousarray(laid["L0_xattn_" + n].T)
    laid["maskT"] = np.ascontiguousarray(laid.pop("mask_BxS_ff1").reshape(NT, P).T)
    for k, n in (("ff_b1", "L0_xattn_ff_b1"), ("bq", "L1_xattn_bq"), ("bk", "L1_xattn_bk"), ("bv", "L1_xattn_bv")):
        laid[k + "_col"] = np.ascontiguousarray(laid[n].reshape(-1, P).T)
    arrays, aps = {}, {}
    for n, v in laid.items():
        arrays["in_" + n] = v
        aps[n] = nc.dram_tensor("in_" + n, v.shape, mybir.dt.from_np(v.dtype), kind="ExternalInput").ap()
    out = nc.dram_tensor("out", (B, S, D), F32, kind="ExternalOutput").ap()
    program(nc, aps, out)
    return run_bass_kernel_spmd(nc, [arrays], core_ids=[0]).results[0]["out"]
```
